# Optimizing a Trainium2 kernel written in Bass

```python
import numpy as np
import jax
import jax.numpy as jnp

def _softmax(x, axis=-1):
    return jax.nn.softmax(x, axis=axis)

def _gelu(x):
    return jax.nn.gelu(x, approximate=True)

def _silu(x):
    return jax.nn.silu(x)

def _sigmoid(x):
    return jax.nn.sigmoid(x)

def _layernorm(x, axis=-1, eps=1e-05):
    m = jnp.mean(x, axis=axis, keepdims=True)
    v = jnp.var(x, axis=axis, keepdims=True)
    return (x - m) / jnp.sqrt(v + eps)

def _scatter_add(tgt, idx, src, axis=0):
    return tgt.at[idx].add(src)

def _segment_sum(src, seg, n):
    return jax.ops.segment_sum(src, seg, n)
kernel_name = 'mk_xattn_ffn_d1_seqx_r8_5b2e82'

def setup_inputs(seed: int=0):
    np.random.seed(seed)
    _w = jnp.asarray

    def _rec_inputs():
        import jax
        import jax.numpy as jnp
        _rk = jax.random.key(seed)
        x = 7.22e-05 + 1 * jax.random.normal(jax.random.fold_in(_rk, 1), (16, 128, 128), jnp.float32)
        _lenS = 128 - jax.random.randint(jax.random.fold_in(_rk, 7), (16,), 0, max(1, 128 // 4) + 1, jnp.int32)
        _lenS2 = 128 - jax.random.randint(jax.random.fold_in(_rk, 8), (16,), 0, max(1, 128 // 4) + 1, jnp.int32)
        _ctx_1024P = jax.random.normal(jax.random.fold_in(_rk, 11), (16, 16, 128), jnp.float32)
        _ctx_1024c = jax.random.dirichlet(jax.random.fold_in(_rk, 511), 0.3 * jnp.ones((16,), jnp.float32), (16, 128))
        _ctx_1024t = jnp.einsum('bsk,bkd->bsd', _ctx_1024c, _ctx_1024P)
        _ctx_1024t = _ctx_1024t * jax.lax.rsqrt(jnp.mean(jnp.square(_ctx_1024t)) + 1e-12) * 0.953939
        ctx_1024 = 4.13588e-05 + 0.999923 * (_ctx_1024t + 0.3 * jax.random.normal(jax.random.fold_in(_rk, 611), (16, 128, 128), jnp.float32))
        return (x, ctx_1024)
    x, ctx_1024 = _rec_inputs()

    def _L0_xattn_setup():
        import jax, jax.numpy as jnp
        import numpy as np
        B, S, D, H, W = (2, 512, 128, 16, 16)
        HD = D // H
        key = jax.random.key(seed)
        ks = jax.random.split(key, 10)
        std = 0.02
        mk_w = lambda k: jax.random.normal(k, (D, D), jnp.float32) * std
        mk_b = lambda k: jax.random.normal(k, (D,), jnp.float32) * std
        return {'query': jax.random.normal(ks[0], (B, S, D), jnp.float32), 'kv': jax.random.normal(ks[1], (B, S, D), jnp.float32), 'Wq': mk_w(ks[2]), 'bq': mk_b(ks[3]), 'Wk': mk_w(ks[4]), 'bk': mk_b(ks[5]), 'Wv': mk_w(ks[6]), 'bv': mk_b(ks[7]), 'Wo': mk_w(ks[8]), 'bo': mk_b(ks[9]), 'is_causal': 1}
    _L0_xattn_all = _L0_xattn_setup()
    _L0_xattn_in = {k: v for k, v in _L0_xattn_all.items() if k in ('Wq', 'bq', 'Wk', 'bk', 'Wv', 'bv', 'Wo', 'bo')}
    del _L0_xattn_all

    def _L0_ffn_setup():
        import jax, jax.numpy as jnp
        import numpy as np
        B, S, D, H, E, K = (4, 256, 128, 512, 4, 2)
        key = jax.random.key(seed)
        ks = jax.random.split(key, 7)
        s1 = 1.0 / np.sqrt(D)
        s2 = 1.0 / np.sqrt(H)
        return {'x': jax.random.normal(ks[0], (B, S, D), jnp.float32), 'w1': jax.random.uniform(ks[1], (E, D, H), jnp.float32, -s1, s1), 'b1': jax.random.uniform(ks[2], (E, H), jnp.float32, -s1, s1), 'w2': jax.random.uniform(ks[3], (E, H, D), jnp.float32, -s2, s2), 'b2': jax.random.uniform(ks[4], (E, D), jnp.float32, -s2, s2), 'wr': jax.random.uniform(ks[5], (D, E), jnp.float32, -s1, s1), 'br': jax.random.uniform(ks[6], (E,), jnp.float32, -s1, s1)}
    _L0_ffn_all = _L0_ffn_setup()
    _L0_ffn_in = {k: v for k, v in _L0_ffn_all.items() if k in ('w1', 'b1', 'w2', 'b2', 'wr', 'br')}
    del _L0_ffn_all
    return {'x': x, 'ctx_1024': ctx_1024, 'L0_xattn_Wq': _L0_xattn_in['Wq'], 'L0_xattn_bq': _L0_xattn_in['bq'], 'L0_xattn_Wk': _L0_xattn_in['Wk'], 'L0_xattn_bk': _L0_xattn_in['bk'], 'L0_xattn_Wv': _L0_xattn_in['Wv'], 'L0_xattn_bv': _L0_xattn_in['bv'], 'L0_xattn_Wo': _L0_xattn_in['Wo'], 'L0_xattn_bo': _L0_xattn_in['bo'], 'L0_ffn_w1': _L0_ffn_in['w1'], 'L0_ffn_b1': _L0_ffn_in['b1'], 'L0_ffn_w2': _L0_ffn_in['w2'], 'L0_ffn_b2': _L0_ffn_in['b2'], 'L0_ffn_wr': _L0_ffn_in['wr'], 'L0_ffn_br': _L0_ffn_in['br']}

def reference(x, ctx_1024, L0_xattn_Wq, L0_xattn_bq, L0_xattn_Wk, L0_xattn_bk, L0_xattn_Wv, L0_xattn_bv, L0_xattn_Wo, L0_xattn_bo, L0_ffn_w1, L0_ffn_b1, L0_ffn_w2, L0_ffn_b2, L0_ffn_wr, L0_ffn_br):
    import jax
    import jax.numpy as jnp

    def _L0_xattn_ref(query, kv, Wq, bq, Wk, bk, Wv, bv, Wo, bo, is_causal):
        import jax, jax.numpy as jnp
        import numpy as np
        B, S, D, H, W = (2, 512, 128, 16, 16)
        HD = D // H
        b, s, d = query.shape

        def split_heads(x):
            return x.reshape(b, s, H, HD).transpose(0, 2, 1, 3)
        Q = split_heads(query @ Wq.T + bq)
        K = split_heads(kv @ Wk.T + bk)
        V = split_heads(kv @ Wv.T + bv)
        pad = W - 1
        Kp = jnp.pad(K, ((0, 0), (0, 0), (pad, 0), (0, 0)))
        Vp = jnp.pad(V, ((0, 0), (0, 0), (pad, 0), (0, 0)))
        idx = jnp.arange(s)[:, None] + jnp.arange(W)[None, :]
        Kw = Kp[:, :, idx]
        Vw = Vp[:, :, idx]
        scores = jnp.einsum('bhsd,bhswd->bhsw', Q, Kw) / np.sqrt(HD).astype(np.float32)
        if is_causal:
            mask = jnp.arange(W)[None, :] <= jnp.arange(s)[:, None]
            scores = jnp.where(mask[None, None], scores, -jnp.inf)
        attn = jax.nn.softmax(scores, axis=-1)
        out = jnp.einsum('bhsw,bhswd->bhsd', attn, Vw)
        out = out.transpose(0, 2, 1, 3).reshape(b, s, d)
        return out @ Wo.T + bo

    def _L0_ffn_ref(x, w1, b1, w2, b2, wr, br):
        import jax, jax.numpy as jnp
        import numpy as np
        B, S, D, H, E, K = (4, 256, 128, 512, 4, 2)
        Bx, Sx, Dx = x.shape
        xf = x.reshape(-1, Dx)
        logits = xf @ wr + br
        topk_vals, topk_idx = jax.lax.top_k(logits, K)
        gates = jax.nn.softmax(topk_vals, axis=-1)
        h = jax.nn.gelu(jnp.einsum('nd,edh->enh', xf, w1) + b1[:, None, :], approximate=False)
        y = jnp.einsum('enh,ehd->end', h, w2) + b2[:, None, :]
        c = jnp.einsum('eh,ehd->ed', jax.nn.gelu(b1, approximate=False), w2) + b2
        c_sum = c.sum(axis=0)
        yt = jnp.transpose(y, (1, 0, 2))
        y_sel = jnp.take_along_axis(yt, topk_idx[:, :, None], axis=1)
        c_sel = c[topk_idx]
        out = jnp.einsum('nk,nkd->nd', gates, y_sel - c_sel + c_sum[None, None, :])
        return out.reshape(Bx, Sx, Dx)
    x = x + _L0_xattn_ref(_layernorm(x, axis=-1), ctx_1024, L0_xattn_Wq, L0_xattn_bq, L0_xattn_Wk, L0_xattn_bk, L0_xattn_Wv, L0_xattn_bv, L0_xattn_Wo, L0_xattn_bo, 1)
    x = x + _L0_ffn_ref(_layernorm(x, axis=-1), L0_ffn_w1, L0_ffn_b1, L0_ffn_w2, L0_ffn_b2, L0_ffn_wr, L0_ffn_br)
    return x

_drawn_inputs = setup_inputs


def setup_inputs(seed=0):
    import zlib

    import numpy as np

    out = dict(_drawn_inputs(seed))
    spreads = {}
    factors = {'L0_xattn_Wq': 8.0,
     'L0_xattn_bq': 64.0,
     'L0_xattn_Wk': 8.0,
     'L0_xattn_bk': 64.0,
     'L0_xattn_bv': 8.0}
    for name, (base, spread) in spreads.items():
        noise = np.random.default_rng([zlib.crc32(name.encode()), seed]).standard_normal(out[name].shape)
        drawn = base * np.exp(spread * noise) if base else spread * noise
        out[name] = jnp.asarray(drawn.astype(out[name].dtype))
    for name, factor in factors.items():
        out[name] = (out[name] * factor).astype(out[name].dtype)
    return out
```

```python
import concourse.bass as bass
from concourse import mybir
from contextlib import ExitStack

B, S, D = 16, 128, 128
H, HD, W = 16, 8, 16
E, F = 4, 512
P = 128
EPS = 1e-5

CB = 4
CT = CB * S
CHUNKS = B // CB
QB = 16
KW = 2 * QB
NQB = S // QB
QUADS = NQB // 4
SP_ = QB + S
HG = H // 2
NC = 4
VW = 2 * HD + 1
HC = F // P
NK = E * HC
HRING = 8
FRING = 4


def xattn_ffn_kernel(nc, x, ctxT, wqkvo, w1, w2, pcols, wr, consts, out):
    fp32 = mybir.dt.float32
    f32r = mybir.dt.float32r
    bf16 = mybir.dt.bfloat16
    ALU = mybir.AluOpType
    ACT = mybir.ActivationFunctionType
    X = mybir.AxisListType.X

    with ExitStack() as stack:
        def sb(name, shape, dt=fp32):
            return stack.enter_context(nc.sbuf_tensor(name, shape, dt))

        def sem(name):
            return stack.enter_context(nc.semaphore(name))

        wa = sb("wa", [P, 4, D])
        wa_hi, wa_lo = sb("wa_hi", [P, 4, D], f32r), sb("wa_lo", [P, 4, D], f32r)
        w2_raw = sb("w2_raw", [P, NK * P])
        h_f = sb("h_f", [P, FRING, CT])
        w1_raw = h_f[:, :, :].rearrange("p r t -> p (r t)")
        w1_hi, w1_lo = sb("w1_hi", [P, NK, P], f32r), sb("w1_lo", [P, NK, P], f32r)
        w2_hi, w2_lo = sb("w2_hi", [P, NK, P], f32r), sb("w2_lo", [P, NK, P], f32r)
        cols = sb("cols", [P, 28])
        wr_raw, wr_hi, wr_lo = sb("wr_raw", [P, E]), sb("wr_hi", [P, E], f32r), sb("wr_lo", [P, E], f32r)
        cst = sb("cst", [P, 128 + 2 + 16 + 128 + 512])
        ident = cst[:, 0:128]
        first_head, second_head = cst[:, 128:129], cst[:, 129:130]
        lower = cst[:, 130:146].rearrange("p (e j) -> p e j", e=E)
        mask_l, mask_r = sb("mask_l", [KW, P], bf16), sb("mask_r", [KW, CT], bf16)
        bq, bk, bv, bo = (cols[:, i:i + 1] for i in range(4))
        b1c, b2c, brc = cols[:, 4:20], cols[:, 20:24], cols[0:E, 24:25]
        neg_half = sb("neg_half", [P, CB])
        gelu_b1 = sb("gelu_b1", [P, NK])
        csum, kappa = sb("csum", [P, 2]), sb("kappa", [P, E])

        x_all = sb("x_all", [P, B, D])
        ctx = sb("ctx", [P, CT])
        fence = sb("fence", [P, 2])
        stats, mv = sb("stats", [P, CB, 6]), sb("mv", [P, CB, 2])
        veps, rstd = sb("veps", [P, CB]), sb("rstd", [P, CB])
        xn = sb("xn", [P, CB, D])
        xt_hi, xt_lo = sb("xt_hi", [P, CT], f32r), sb("xt_lo", [P, CT], f32r)
        ct_hi, ct_lo = sb("ct_hi", [P, CT], f32r), sb("ct_lo", [P, CT], f32r)
        qT = sb("qT", [P, CT])
        q_exp = sb("q_exp", [P, H, CT])
        kT, vT = sb("kT", [P, CB, SP_]), sb("vT", [P, CB, SP_])
        v_diag = sb("v_diag", [P, CB * NQB, 2, VW])
        v_exp = sb("v_exp", [P, NC, CB * NQB, 2, VW])
        sT = sb("sT", [P, CT])
        smax = sb("smax", [P, 16])
        shifted, p_exp, pT = sb("shifted", [P, CT]), sb("p_exp", [P, CT]), sb("pT", [P, CT])
        rden = sb("rden", [P, 16])
        att = sb("att", [P, 2 * D])
        half = sb("half", [P, S])
        aT = sb("aT", [P, CT])
        at_hi, at_lo = sb("at_hi", [P, CT], f32r), sb("at_lo", [P, CT], f32r)
        oT = sb("oT", [P, CT])
        x1 = sb("x1", [P, CB, D])
        x2_hi, x2_lo = sb("x2_hi", [P, CT], f32r), sb("x2_lo", [P, CT], f32r)
        lgT = sb("lgT", [P, CT])
        lg, lgs, lge = sb("lg", [P, CB, E]), sb("lgs", [P, CB, E]), sb("lge", [P, CB, E])
        lmax = sb("lmax", [P, CB])
        gt, eq = sb("gt", [P, CB, E, E]), sb("eq", [P, CB, E, E])
        rank, gsel = sb("rank", [P, CB, E]), sb("gsel", [P, CB, E])
        gsum, gate = sb("gsum", [P, CB]), sb("gate", [P, CB, E])
        h_hi, h_lo = sb("h_hi", [P, HRING, CT], f32r), sb("h_lo", [P, HRING, CT], f32r)
        yT = sb("yT", [P, CT])

        banks = [stack.enter_context(nc.psum_tensor(f"bank{i}", [P, 512], fp32)) for i in range(8)]
        gen0, gen1, ps_s, ps_t, ps_o, h0, h1, ps_y = banks
        ps_h = [h0, h1]

        ld_attn, ld_x, ld_ctx, ld_w1, ld_w2 = (sem(n) for n in ("ld_attn", "ld_x", "ld_ctx", "ld_w1", "ld_w2"))
        zeroed, wa_split, w1_split, w2_split = (sem(n) for n in ("zeroed", "wa_split", "w1_split", "w2_split"))
        wa_hi_ready, w1_hi_ready, w2_hi_ready = (sem(n) for n in ("wa_hi_ready", "w1_hi_ready", "w2_hi_ready"))
        gelu_b1_ready, d_psum, kappa_ready = (sem(n) for n in ("gelu_b1_ready", "d_psum", "kappa_ready"))
        dve_chain, pool_chain = sem("dve_chain"), sem("pool_chain")
        var_ready, rstd_ready, xn_ready, xT_psum = (sem(n) for n in ("var_ready", "rstd_ready", "xn_ready", "xT_psum"))
        xhi_ready, xlo_ready, chi_ready, clo_ready = (sem(n) for n in ("xhi_ready", "xlo_ready", "chi_ready", "clo_ready"))
        q_psum, k_psum, v_psum = (sem(n) for n in ("q_psum", "k_psum", "v_psum"))
        qT_ready, kT_ready, vT_ready = (sem(n) for n in ("qT_ready", "kT_ready", "vT_ready"))
        qexp_loaded, vdiag_ready, vexp_loaded = (sem(n) for n in ("qexp_loaded", "vdiag_ready", "vexp_loaded"))
        s_psum, sT_ready, sc_psum, shifted_ready = (sem(n) for n in ("s_psum", "sT_ready", "sc_psum", "shifted_ready"))
        p_ready, pT_ready, o_psum, att_ready = (sem(n) for n in ("p_ready", "pT_ready", "o_psum", "att_ready"))
        at_psum, half_ready, aT_ready = (sem(n) for n in ("at_psum", "half_ready", "aT_ready"))
        ahi_ready, alo_ready, proj_psum, oT_ready, back_psum = (
            sem(n) for n in ("ahi_ready", "alo_ready", "proj_psum", "oT_ready", "back_psum"))
        lgT_psum, lgT_ready, lg_psum, lgs_ready, lge_ready, gate_ready = (
            sem(n) for n in ("lgT_psum", "lgT_ready", "lg_psum", "lgs_ready", "lge_ready", "gate_ready"))
        h_psum, h_ready, hhi_ready, hlo_ready, h_used = (
            sem(n) for n in ("h_psum", "h_ready", "hhi_ready", "hlo_ready", "h_used"))
        yT_ready, yt_psum, y_added, out_stored = (
            sem(n) for n in ("yT_ready", "yt_psum", "y_added", "out_stored"))

        block = stack.enter_context(nc.Block())

        @block.sync
        def _(sp):
            sp.dma_start(cst[:, :], consts).then_inc(ld_attn, 16)
            sp.dma_start(cols[:, :], pcols).then_inc(ld_attn, 16)
            sp.dma_start(wr_raw[:, :], wr).then_inc(ld_attn, 16)
            sp.dma_start(wa[:, :, :], wqkvo).then_inc(ld_attn, 16)
            sp.dma_start(x_all[:, :, :], x.rearrange("b s d -> s b d")).then_inc(ld_x, 16)
            sp.dma_start(w1_raw[:, :], w1).then_inc(ld_w1, 16)
            sp.dma_start(w2_raw[:, :], w2).then_inc(ld_w2, 16)
            sp.wait_ge(zeroed, 1)

            with sp.Fori(0, CHUNKS) as c:
                done_batches, done_heads, experts = sp.snap(c * CB), sp.snap(c + 1), sp.snap(c * E + E)
                first_token = sp.snap(c * CT)
                sp.wait_ge(clo_ready, c)
                sp.dma_start(ctx[:, :], ctxT[:, bass.ds(first_token, CT)]).then_inc(ld_ctx, 16)
                sp.wait_ge(qT_ready, done_heads)
                for h in range(H):
                    sp.dma_start(q_exp[HD * h:HD * (h + 1), h, :], qT[HD * h:HD * (h + 1), :]).then_inc(qexp_loaded, 16)
                sp.wait_ge(vdiag_ready, done_heads)
                for q in range(NC):
                    sp.dma_start(v_exp[32 * q:32 * (q + 1), q, :, :, :],
                                 v_diag[32 * q:32 * (q + 1), :, :, :]).then_inc(vexp_loaded, 16)
                sp.wait_ge(y_added, experts)
                sp.dma_start(out[bass.ds(done_batches, CB), :, :].rearrange("b s d -> s b d"), x1[:, :, :]).then_inc(out_stored, 16)
            sp.wait_ge(out_stored, CHUNKS * 16)

        @block.gpsimd
        def _(pool):
            nc.gpsimd.memset(kT[:, :, 0:QB], 0.0)
            nc.gpsimd.memset(vT[:, :, 0:QB], 0.0)
            nc.gpsimd.memset(lgT[:, :], 0.0)
            nc.gpsimd.memset(neg_half[:, :], -0.5)
            nc.gpsimd.memset(v_diag[:, :, :, :], 1.0)
            nc.gpsimd.memset(q_exp[:, :, :], 0.0)
            nc.gpsimd.memset(v_exp[:, :, :, :, :], 0.0).then_inc(zeroed, 1)

            def inverse_deviation(n):
                pool.wait_ge(var_ready, n + 1)
                nc.gpsimd.tensor_tensor(rstd[:, :], veps[:, :], neg_half[:, :], ALU.pow).then_inc(rstd_ready, 1)

            pool.wait_ge(zeroed, 1)
            with pool.Fori(0, CHUNKS) as c:
                inverse_deviation(c * 2)
                pool.wait_ge(chi_ready, c + 1)
                nc.gpsimd.tensor_tensor(ct_lo[:, :], ctx[:, :], ct_hi[:, :].bitcast(fp32), ALU.subtract).then_inc(clo_ready, 1)
                inverse_deviation(c * 2 + 1)

        @block.scalar
        def _(act):
            Id = ACT.Identity
            act.wait_ge(ld_attn, 64)
            nc.scalar.activation(wa_hi[:, :, :], wa[:, :, :], ACT.Copy)
            nc.scalar.activation(wr_hi[:, :], wr_raw[:, :], ACT.Copy)
            nc.scalar.activation(mask_l[:, :], cst[0:KW, 146:274], ACT.Copy)
            nc.scalar.activation(mask_r[:, :], cst[0:KW, 274:786], ACT.Copy)
            nc.scalar.activation(gelu_b1[:, :], b1c, ACT.Gelu).then_inc(wa_hi_ready, 1)
            act.wait_ge(ld_w1, 16)
            nc.scalar.activation(w1_hi[:, :, :].rearrange("p k m -> p (k m)"), w1_raw[:, :], ACT.Copy).then_inc(w1_hi_ready, 1)
            act.wait_ge(ld_w2, 16)
            nc.scalar.activation(w2_hi[:, :, :].rearrange("p k m -> p (k m)"), w2_raw[:, :], ACT.Copy).then_inc(w2_hi_ready, 1)
            act.wait_ge(zeroed, 1)

            def split_x(n, bank, hi, free):
                act.wait_ge(xT_psum, n + 1)
                nc.scalar.activation(hi[:, :], bank[:, :], ACT.Copy).then_inc(xhi_ready, 1)

            def project_in(c):
                act.wait_ge(ld_ctx, c * 16 + 16)
                act.wait_ge(v_psum, c)
                nc.scalar.activation(ct_hi[:, :], ctx[:, :], ACT.Copy).then_inc(chi_ready, 1)
                split_x(c * 2, gen0, xt_hi, None)
                act.wait_ge(q_psum, c + 1)
                act.wait_ge(qexp_loaded, c * 16 * H)
                act.wait_ge(s_psum, c * CB)
                nc.scalar.activation(qT[:, :], gen1[:, :], Id, bias=bq).then_inc(qT_ready, 1)
                act.wait_ge(k_psum, c + 1)
                nc.scalar.activation(kT[:, :, QB:SP_], gen0[:, :].rearrange("p (b s) -> p b s", b=CB), Id,
                                     bias=bk).then_inc(kT_ready, 1)
                act.wait_ge(v_psum, c + 1)
                nc.scalar.activation(vT[:, :, QB:SP_], gen1[:, :].rearrange("p (b s) -> p b s", b=CB), Id,
                                     bias=bv).then_inc(vT_ready, 1)

            def scores_out(n):
                act.wait_ge(s_psum, n + 1)
                act.wait_ge(sc_psum, n)
                nc.scalar.activation(sT[:, :], ps_s[:, :], ACT.Copy).then_inc(sT_ready, 1)

            def exponent(n):
                act.wait_ge(shifted_ready, n + 1)
                act.wait_ge(pT_ready, n)
                nc.scalar.activation(p_exp[:, :], shifted[:, :], ACT.Exp, scale=float(HD) ** -0.5).then_inc(p_ready, 1)

            def first_half(n):
                act.wait_ge(at_psum, n + 1)
                act.wait_ge(aT_ready, n)
                nc.scalar.activation(half[:, :].rearrange("p (g q) -> p g q", q=QB),
                                     ps_t[:, 0:2 * S].rearrange("p (g i q) -> p g i q", i=2, q=QB)[:, :, 0, :],
                                     ACT.Copy, scale=first_head).then_inc(half_ready, 1)

            def project_out(c):
                act.wait_ge(aT_ready, c * CB + CB)
                nc.scalar.activation(at_hi[:, :], aT[:, :], ACT.Copy).then_inc(ahi_ready, 1)
                act.wait_ge(proj_psum, c + 1)
                nc.scalar.activation(oT[:, :], gen0[:, :], Id, bias=bo).then_inc(oT_ready, 1)
                split_x(c * 2 + 1, gen0, x2_hi, None)
                act.wait_ge(lgT_psum, c + 1)
                nc.scalar.activation(lgT[0:E, :], gen1[0:E, :], Id, bias=brc).then_inc(lgT_ready, 1)
                act.wait_ge(lgs_ready, c + 1)
                nc.scalar.activation(lge[:, :, :], lgs[:, :, :], ACT.Exp).then_inc(lge_ready, 1)

            def hidden(c, k):
                act.wait_ge(h_psum, c * NK + k + 1)
                act.wait_ge(hlo_ready, c * NK + max(k + 1 - FRING, 0))
                nc.scalar.activation(h_f[:, k % FRING, :], ps_h[k % 2][:, :], ACT.Gelu,
                                     bias=b1c[:, k:k + 1]).then_inc(h_ready, 1)
                act.wait_ge(h_ready, c * NK + k + 1)
                act.wait_ge(h_used, c * NK + max(k + 1 - HRING, 0))
                nc.scalar.activation(h_hi[:, k % HRING, :], h_f[:, k % FRING, :], ACT.Copy).then_inc(hhi_ready, 1)

            def expert_out(c, e):
                act.wait_ge(h_used, c * NK + (e + 1) * HC)
                act.wait_ge(yt_psum, c * E + e)
                nc.scalar.activation(yT[:, :], ps_y[:, :], Id, bias=kappa[:, e:e + 1]).then_inc(yT_ready, 1)

            act.wait_ge(kappa_ready, 1)
            with act.Fori(0, CHUNKS) as c:
                project_in(c)
                for b in range(CB):
                    n = c * CB + b
                    scores_out(n)
                    exponent(n)
                    first_half(n)
                project_out(c)
                for k in range(NK):
                    hidden(c, k)
                    if k % HC == HC - 1 and k >= HC:
                        expert_out(c, k // HC - 1)
                expert_out(c, E - 1)

        @block.vector
        def _(dve):
            V = nc.vector

            dve.wait_ge(wa_hi_ready, 1)
            V.tensor_tensor(wa_lo[:, :, :], wa[:, :, :], wa_hi[:, :, :].bitcast(fp32), ALU.subtract)
            V.tensor_tensor(wr_lo[:, :], wr_raw[:, :], wr_hi[:, :].bitcast(fp32), ALU.subtract).then_inc(wa_split, 1)
            dve.wait_ge(w1_hi_ready, 1)
            V.tensor_tensor(w1_lo[:, :, :].rearrange("p k m -> p (k m)"), w1_raw[:, :],
                            w1_hi[:, :, :].rearrange("p k m -> p (k m)").bitcast(fp32), ALU.subtract).then_inc(w1_split, 1)
            dve.wait_ge(w2_hi_ready, 1)
            V.tensor_tensor(w2_lo[:, :, :].rearrange("p k m -> p (k m)"), w2_raw[:, :],
                            w2_hi[:, :, :].rearrange("p k m -> p (k m)").bitcast(fp32), ALU.subtract).then_inc(w2_split, 1)
            dve.wait_ge(d_psum, 1)
            V.tensor_reduce(csum[:, 0:1], ps_y[:, 0:E], X, ALU.add)
            V.tensor_reduce(csum[:, 1:2], b2c, X, ALU.add).then_inc(dve_chain, 1)
            dve.wait_ge(dve_chain, 1)
            V.tensor_tensor(csum[:, 0:1], csum[:, 0:1], csum[:, 1:2], ALU.add).then_inc(dve_chain, 1)
            dve.wait_ge(dve_chain, 2)
            V.tensor_scalar(kappa[:, :], ps_y[:, 0:E], -1.0, csum[:, 0:1], ALU.mult, ALU.add).then_inc(kappa_ready, 1)
            dve.wait_ge(kappa_ready, 1)
            dve.wait_ge(ld_x, 16)

            SETUP = 2
            LN_LINKS, BATCH_LINKS, GATE_LINKS = 2, 2, 9
            LINKS = LN_LINKS + CB * BATCH_LINKS + 1 + LN_LINKS + GATE_LINKS

            def link(ins, value):
                ins.then_inc(dve_chain, 1)
                dve.wait_ge(dve_chain, value)

            def layer_norm(n, src, at):
                for b in range(CB):
                    last = V.bn_stats(stats[:, b, :], src[b])
                link(last, at + 1)
                V.memset(fence[:, 0:1], 0.0)
                for b in range(CB):
                    last = V.bn_aggr(mv[:, b, :], stats[:, b, :])
                link(last, at + 2)
                V.tensor_scalar(veps[:, :], mv[:, :, 1], EPS, None, ALU.add).then_inc(var_ready, 1)
                dve.wait_ge(rstd_ready, n + 1)
                dve.wait_ge(xT_psum, n)
                for b in range(CB):
                    last = V.tensor_scalar(xn[:, b, :], src[b], mv[:, b, 0:1], rstd[:, b:b + 1],
                                           ALU.subtract, ALU.mult)
                last.then_inc(xn_ready, 1)

            def values_in(c):
                dve.wait_ge(vT_ready, c + 1)
                dve.wait_ge(vexp_loaded, c * 16 * NC)
                dve.wait_ge(o_psum, c * CB)
                for b in range(CB):
                    last = V.transpose(v_diag[:, b * NQB:(b + 1) * NQB, :, 0:2 * HD], windows(vT, b))
                last.then_inc(vdiag_ready, 1)

            def windows(t, b):
                a = t[:, b, 0:KW]
                return bass.AP(a.tensor, a.offset, [list(a.ap[0]), [QB, NQB], [1, KW]])

            def split_lo(n, bank, hi, lo):
                dve.wait_ge(xhi_ready, n + 1)
                V.tensor_tensor(lo[:, :], bank[:, :], hi[:, :].bitcast(fp32), ALU.subtract).then_inc(xlo_ready, 1)

            def softmax(n, at):
                dve.wait_ge(sc_psum, n + 1)
                blocks = ps_t[:, :].rearrange("p (g k) -> p g k", k=KW)
                link(V.tensor_reduce(smax[:, :], blocks, X, ALU.max), at + 1)
                dve.wait_ge(p_ready, n)
                V.tensor_tensor(shifted[:, :].rearrange("p (g k) -> p g k", k=KW), blocks,
                                smax[:, :, None].to_broadcast([P, 16, KW]), ALU.subtract).then_inc(shifted_ready, 1)

            def probabilities(n):
                dve.wait_ge(p_ready, n + 1)
                dve.wait_ge(o_psum, n)
                V.transpose(pT[:, :], p_exp[:, :]).then_inc(pT_ready, 1)

            def normalize(n, at):
                dve.wait_ge(o_psum, n + 1)
                o = ps_o[:, 0:16 * VW].rearrange("p (g v) -> p g v", v=VW)
                link(V.reciprocal(rden[:, :], o[:, :, 2 * HD]), at + 1)
                dve.wait_ge(at_psum, n)
                V.tensor_tensor(att[:, :].rearrange("p (g v) -> p g v", v=2 * HD), o[:, :, 0:2 * HD],
                                rden[:, :, None].to_broadcast([P, 16, 2 * HD]), ALU.mult).then_inc(att_ready, 1)

            def second_half(n, b):
                dve.wait_ge(half_ready, n + 1)
                V.scalar_tensor_tensor(aT[:, b * S:(b + 1) * S].rearrange("p (g q) -> p g q", q=QB),
                                       ps_t[:, 0:2 * S].rearrange("p (g i q) -> p g i q", i=2, q=QB)[:, :, 1, :],
                                       second_head, half[:, :].rearrange("p (g q) -> p g q", q=QB),
                                       ALU.mult, ALU.add).then_inc(aT_ready, 1)

            def gates(c, at):
                dve.wait_ge(lg_psum, c + 1)
                link(V.tensor_copy(lg[:, :, :], gen0[:, :].rearrange("p (b e) -> p b e", b=CB)[:, :, 0:E]), at + 1)
                link(V.tensor_reduce(lmax[:, :], lg[:, :, :], X, ALU.max), at + 2)
                V.tensor_tensor(lgs[:, :, :], lg[:, :, :], lmax[:, :, None].to_broadcast([P, CB, E]),
                                ALU.subtract).then_inc(lgs_ready, 1)
                others = lg[:, :, None, :].to_broadcast([P, CB, E, E])
                own = lg[:, :, :, None].to_broadcast([P, CB, E, E])
                V.tensor_tensor(gt[:, :, :, :], others, own, ALU.is_gt)
                link(V.tensor_tensor(eq[:, :, :, :], others, own, ALU.is_equal), at + 3)
                link(V.tensor_tensor(eq[:, :, :, :], eq[:, :, :, :], lower[:, None, :, :].to_broadcast([P, CB, E, E]),
                                     ALU.mult), at + 4)
                link(V.tensor_tensor(gt[:, :, :, :], gt[:, :, :, :], eq[:, :, :, :], ALU.add), at + 5)
                link(V.tensor_reduce(rank[:, :, :], gt[:, :, :, :], X, ALU.add), at + 6)
                dve.wait_ge(lge_ready, c + 1)
                link(V.scalar_tensor_tensor(gsel[:, :, :], rank[:, :, :], 2.0, lge[:, :, :], ALU.is_lt, ALU.mult), at + 7)
                link(V.tensor_reduce(gsum[:, :], gsel[:, :, :], X, ALU.add), at + 8)
                link(V.reciprocal(gsum[:, :], gsum[:, :]), at + 9)
                V.tensor_tensor(gate[:, :, :], gsel[:, :, :], gsum[:, :, None].to_broadcast([P, CB, E]),
                                ALU.mult).then_inc(gate_ready, 1)

            def hidden_lo(c, k):
                dve.wait_ge(hhi_ready, c * NK + k + 1)
                V.tensor_tensor(h_lo[:, k % HRING, :], h_f[:, k % FRING, :], h_hi[:, k % HRING, :].bitcast(fp32),
                                ALU.subtract).then_inc(hlo_ready, 1)

            def add_expert(c, e):
                dve.wait_ge(yt_psum, c * E + e + 1)
                dve.wait_ge(gate_ready, c + 1)
                dve.wait_ge(y_added, c * E + e)
                for b in range(CB):
                    last = V.scalar_tensor_tensor(x1[:, b, :], ps_y[:, b * S:(b + 1) * S], gate[:, b, e:e + 1],
                                                  x1[:, b, :], ALU.mult, ALU.add)
                last.then_inc(y_added, 1)

            with dve.Fori(0, CHUNKS) as c:
                at = c * LINKS + SETUP
                layer_norm(c * 2, [x_all[:, bass.ds(c * CB + b, 1), :].rearrange("p o d -> p (o d)") for b in range(CB)], at)
                split_lo(c * 2, gen0, xt_hi, xt_lo)
                values_in(c)
                at = at + 2
                for b in range(CB):
                    n = c * CB + b
                    softmax(n, at + 2 * b)
                    probabilities(n)
                    normalize(n, at + 2 * b + 1)
                    second_half(n, b)
                at = at + 2 * CB
                dve.wait_ge(ahi_ready, c + 1)
                V.tensor_tensor(at_lo[:, :], aT[:, :], at_hi[:, :].bitcast(fp32), ALU.subtract).then_inc(alo_ready, 1)
                dve.wait_ge(back_psum, c + 1)
                dve.wait_ge(out_stored, c * 16)
                link(V.tensor_tensor(x1[:, :, :], gen1[:, :].rearrange("p (b d) -> p b d", b=CB),
                                     x_all[:, bass.ds(c * CB, CB), :], ALU.add), at + 1)
                layer_norm(c * 2 + 1, [x1[:, b, :] for b in range(CB)], at + 1)
                split_lo(c * 2 + 1, gen0, x2_hi, x2_lo)
                gates(c, at + 3)
                for k in range(NK):
                    hidden_lo(c, k)
                    if k % HC == HC - 1 and k >= HC:
                        add_expert(c, k // HC - 1)
                add_expert(c, E - 1)
            

        @block.tensor
        def _(pe):
            mm = nc.tensor.matmul

            def split_mm(ps, w_hi, w_lo, r_hi, r_lo, start=True, stop=True):
                mm(ps, w_hi, r_hi, start=start, stop=False)
                mm(ps, w_hi, r_lo, start=False, stop=False)
                return mm(ps, w_lo, r_hi, start=False, stop=stop)

            def transposes(bank, src, width=P):
                for b in range(CB):
                    last = nc.tensor.transpose(bank[:, b * P:(b + 1) * P], src(b), ident)
                return last

            def setup():
                pe.wait_ge(wa_hi_ready, 1)
                pe.wait_ge(ld_w2, 16)
                for e in range(E):
                    for k in range(HC):
                        i = e * HC + k
                        last = mm(ps_y[:, e:e + 1], w2_raw[:, i * P:(i + 1) * P], gelu_b1[:, i:i + 1],
                                  start=(k == 0), stop=(k == HC - 1))
                last.then_inc(d_psum, 1)

            def project_in(c):
                pe.wait_ge(xn_ready, c * 2 + 1)
                pe.wait_ge(gate_ready, c)
                transposes(gen0, lambda b: xn[:, b, :]).then_inc(xT_psum, 1)
                pe.wait_ge(xlo_ready, c * 2 + 1)
                pe.wait_ge(lgT_ready, c)
                split_mm(gen1[:, :], wa_hi[:, 0, :], wa_lo[:, 0, :], xt_hi[:, :], xt_lo[:, :]).then_inc(q_psum, 1)
                pe.wait_ge(clo_ready, c + 1)
                split_mm(gen0[:, :], wa_hi[:, 1, :], wa_lo[:, 1, :], ct_hi[:, :], ct_lo[:, :]).then_inc(k_psum, 1)
                pe.wait_ge(qT_ready, c + 1)
                split_mm(gen1[:, :], wa_hi[:, 2, :], wa_lo[:, 2, :], ct_hi[:, :], ct_lo[:, :]).then_inc(v_psum, 1)

            def scores(c, b, n):
                if b == 0:
                    pe.wait_ge(kT_ready, c + 1)
                    pe.wait_ge(qexp_loaded, (c + 1) * 16 * H)
                pe.wait_ge(sT_ready, n)
                mm(ps_s[:, :], mask_l[:, :], mask_r[:, :], start=True, stop=False, skip_group_check=True)
                for quad in range(QUADS):
                    for j in range(4):
                        t = QB * (4 * quad + j)
                        last = mm(ps_s[32 * j:32 * (j + 1), quad * 256:(quad + 1) * 256], kT[:, b, t:t + KW],
                                  q_exp[:, :, b * S + t:b * S + t + QB], start=False, stop=True,
                                  skip_group_check=True)
                last.then_inc(s_psum, 1)

            def score_rows(n):
                pe.wait_ge(sT_ready, n + 1)
                pe.wait_ge(aT_ready, n)
                transposes(ps_t, lambda i: sT[:, i * P:(i + 1) * P]).then_inc(sc_psum, 1)

            def attend(c, b, n):
                if b == 0:
                    pe.wait_ge(vexp_loaded, (c + 1) * 16 * NC)
                pe.wait_ge(pT_ready, n + 1)
                pe.wait_ge(att_ready, n)
                for quad in range(QUADS):
                    for g in range(2):
                        for j in range(4):
                            i = quad * 2 + g
                            last = mm(ps_o[32 * j:32 * (j + 1), i * NC * VW:(i + 1) * NC * VW],
                                      pT[:, (4 * i + j) * KW:(4 * i + j + 1) * KW],
                                      v_exp[:, :, b * NQB + 4 * quad + j, g, :], start=True, stop=True,
                                      skip_group_check=True)
                last.then_inc(o_psum, 1)

            def attention_columns(n):
                pe.wait_ge(att_ready, n + 1)
                for quad in range(QUADS):
                    last = nc.tensor.transpose(ps_t[:, quad * P:(quad + 1) * P], att[:, quad * P:(quad + 1) * P], ident)
                last.then_inc(at_psum, 1)

            def project_out(c):
                pe.wait_ge(alo_ready, c + 1)
                pe.wait_ge(kT_ready, c + 1)
                split_mm(gen0[:, :], wa_hi[:, 3, :], wa_lo[:, 3, :], at_hi[:, :], at_lo[:, :]).then_inc(proj_psum, 1)
                pe.wait_ge(oT_ready, c + 1)
                pe.wait_ge(vT_ready, c + 1)
                transposes(gen1, lambda b: oT[:, b * P:(b + 1) * P]).then_inc(back_psum, 1)
                pe.wait_ge(xn_ready, c * 2 + 2)
                transposes(gen0, lambda b: xn[:, b, :]).then_inc(xT_psum, 1)
                pe.wait_ge(xlo_ready, c * 2 + 2)
                split_mm(gen1[0:E, :], wr_hi[:, :], wr_lo[:, :], x2_hi[:, :], x2_lo[:, :]).then_inc(lgT_psum, 1)
                pe.wait_ge(lgT_ready, c + 1)
                transposes(gen0, lambda b: lgT[:, b * P:(b + 1) * P]).then_inc(lg_psum, 1)

            def first_layer(c, k):
                pe.wait_ge(h_ready, c * NK + max(k - 1, 0))
                split_mm(ps_h[k % 2][:, :], w1_hi[:, k, :], w1_lo[:, k, :], x2_hi[:, :], x2_lo[:, :]).then_inc(h_psum, 1)

            def second_layer(c, k):
                e = k // HC
                pe.wait_ge(hlo_ready, c * NK + k + 1)
                if k % HC == 0:
                    pe.wait_ge(y_added, c * E + e)
                r = k % HRING
                last = split_mm(ps_y[:, :], w2_hi[:, k, :], w2_lo[:, k, :], h_hi[:, r, :], h_lo[:, r, :],
                                start=(k % HC == 0), stop=(k % HC == HC - 1))
                last.then_inc(h_used, 1)

            def expert_rows(c, e):
                pe.wait_ge(yT_ready, c * E + e + 1)
                transposes(ps_y, lambda b: yT[:, b * P:(b + 1) * P]).then_inc(yt_psum, 1)

            setup()
            pe.wait_ge(wa_split, 1)
            pe.wait_ge(w1_split, 1)
            pe.wait_ge(w2_split, 1)
            pe.wait_ge(kappa_ready, 1)
            with pe.Fori(0, CHUNKS) as c:
                project_in(c)
                for b in range(CB):
                    n = c * CB + b
                    scores(c, b, n)
                    score_rows(n)
                    attend(c, b, n)
                    attention_columns(n)
                project_out(c)
                for k in range(HC):
                    first_layer(c, k)
                for k in range(NK):
                    if k + HC < NK:
                        first_layer(c, k + HC)
                    second_layer(c, k)
                    if k % HC == HC - 1:
                        expert_rows(c, k // HC)


_SHAPES = {"x": (B, S, D), "ctxT": (D, B * S), "wqkvo": (D, 4, D), "w1": (D, NK * P), "w2": (P, NK * D),
           "pcols": (P, 28), "wr": (D, E), "consts": (P, 786)}


def constants():
    import numpy as np
    c = np.zeros((P, 786), np.float32)
    c[:, 0:128] = np.eye(P)
    head = (np.arange(P) // HD) % 2
    c[:, 128] = head == 0
    c[:, 129] = head == 1
    c[:, 130:146] = (np.arange(E)[None, :] < np.arange(E)[:, None]).reshape(1, 16)
    for quad in range(QUADS):
        for q in range(QB):
            for j in range(4):
                for k in range(KW):
                    last = min(q + W, 2 * q + 1) if quad == 0 and j == 0 else q + W
                    if not q + 1 <= k <= last:
                        c[quad * QB + q, 146 + j * KW + k] = -1e30
            c[quad * QB + q, 274 + quad * 256 + q + QB * np.arange(H)] = 1.0
    return c


def kernel(**inputs):
    import numpy as np
    import concourse.bacc as bacc
    from concourse import mybir as mb
    from concourse.bass_utils import run_bass_kernel_spmd

    a = {k: np.ascontiguousarray(v) for k, v in inputs.items()}
    order = np.arange(D).reshape(2, NC, 2, HD).transpose(1, 0, 2, 3).reshape(-1)
    wv, bv = a["L0_xattn_Wv"][order, :], a["L0_xattn_bv"][order]
    br = np.zeros(P, np.float32)
    br[:E] = a["L0_ffn_br"]
    arrays = {
        "x": a["x"],
        "ctxT": a["ctx_1024"].transpose(2, 0, 1).reshape(D, B * S),
        "wqkvo": np.stack([a["L0_xattn_Wq"].T, a["L0_xattn_Wk"].T, wv.T, a["L0_xattn_Wo"].T], axis=1),
        "w1": a["L0_ffn_w1"].reshape(E, D, HC, P).transpose(1, 0, 2, 3).reshape(D, NK * P),
        "w2": a["L0_ffn_w2"].reshape(E, HC, P, D).transpose(2, 0, 1, 3).reshape(P, NK * D),
        "pcols": np.concatenate([
            np.stack([a["L0_xattn_bq"], a["L0_xattn_bk"], bv, a["L0_xattn_bo"]], axis=1),
            a["L0_ffn_b1"].reshape(NK, P).T, a["L0_ffn_b2"].T, br[:, None], np.zeros((P, 3), np.float32)], axis=1),
        "wr": a["L0_ffn_wr"],
        "consts": constants(),
    }
    arrays = {k: np.ascontiguousarray(v) for k, v in arrays.items()}
    nc = bacc.Bacc("TRN2", target_bir_lowering=False, num_devices=1)
    aps = [nc.dram_tensor(f"in_{k}", arrays[k].shape, mb.dt.from_np(arrays[k].dtype), kind="ExternalInput").ap()
           for k in _SHAPES]
    out = nc.dram_tensor("out", (B, S, D), mb.dt.float32, kind="ExternalOutput").ap()
    xattn_ffn_kernel(nc, *aps, out)
    r = run_bass_kernel_spmd(nc, [{f"in_{k}": v for k, v in arrays.items()}], core_ids=[0])
    return r.results[0]["out"]
```

```python
import concourse.bass as bass
from concourse import mybir
from contextlib import ExitStack

B, S, D = 16, 128, 128
H, HD, W = 16, 8, 16
E, F = 4, 512
P = 128
EPS = 1e-5

CB = 4
CT = CB * S
CHUNKS = B // CB
QB = 16
KW = 2 * QB
NQB = S // QB
QUADS = NQB // 4
SP_ = QB + S
HG = H // 2
NC = 4
VW = 2 * HD + 1
HC = F // P
NK = E * HC
HRING = 8
FRING = 4


def xattn_ffn_kernel(nc, x, ctxT, wqkvo, w1, w2, pcols, wr, consts, out):
    fp32 = mybir.dt.float32
    f32r = mybir.dt.float32r
    bf16 = mybir.dt.bfloat16
    ALU = mybir.AluOpType
    ACT = mybir.ActivationFunctionType
    X = mybir.AxisListType.X

    with ExitStack() as stack:
        def sb(name, shape, dt=fp32):
            return stack.enter_context(nc.sbuf_tensor(name, shape, dt))

        def sem(name):
            return stack.enter_context(nc.semaphore(name))

        wa = sb("wa", [P, 4, D])
        wa_hi, wa_lo = sb("wa_hi", [P, 4, D], f32r), sb("wa_lo", [P, 4, D], f32r)
        w2_raw = sb("w2_raw", [P, NK * P])
        h_f = sb("h_f", [P, FRING, CT])
        w1_raw = h_f[:, :, :].rearrange("p r t -> p (r t)")
        w1_hi, w1_lo = sb("w1_hi", [P, NK, P], f32r), sb("w1_lo", [P, NK, P], f32r)
        w2_hi, w2_lo = sb("w2_hi", [P, NK, P], f32r), sb("w2_lo", [P, NK, P], f32r)
        cols = sb("cols", [P, 28])
        wr_raw, wr_hi, wr_lo = sb("wr_raw", [P, E]), sb("wr_hi", [P, E], f32r), sb("wr_lo", [P, E], f32r)
        cst = sb("cst", [P, 128 + 2 + 16 + 128 + 512])
        ident = cst[:, 0:128]
        first_head, second_head = cst[:, 128:129], cst[:, 129:130]
        lower = cst[:, 130:146].rearrange("p (e j) -> p e j", e=E)
        mask_l, mask_r = sb("mask_l", [KW, P], bf16), sb("mask_r", [KW, CT], bf16)
        bq, bk, bv, bo = (cols[:, i:i + 1] for i in range(4))
        b1c, b2c, brc = cols[:, 4:20], cols[:, 20:24], cols[0:E, 24:25]
        neg_half = sb("neg_half", [P, CB])
        gelu_b1 = sb("gelu_b1", [P, NK])
        csum, kappa = sb("csum", [P, 2]), sb("kappa", [P, E])

        x_all = sb("x_all", [P, B, D])
        ctx = sb("ctx", [P, CT])
        fence = sb("fence", [P, 2])
        stats = sb("stats", [P, CB, 6])
        mv1, veps1, rstd1 = sb("mv1", [P, CB, 2]), sb("veps1", [P, CB]), sb("rstd1", [P, CB])
        mv2, veps2, rstd2 = sb("mv2", [P, CB, 2]), sb("veps2", [P, CB]), sb("rstd2", [P, CB])
        xn1, xn2 = sb("xn1", [P, CB, D]), sb("xn2", [P, CB, D])
        xt_hi, xt_lo = sb("xt_hi", [P, CT], f32r), sb("xt_lo", [P, CT], f32r)
        ct_hi, ct_lo = sb("ct_hi", [P, CT], f32r), sb("ct_lo", [P, CT], f32r)
        qT = sb("qT", [P, CT])
        q_exp = sb("q_exp", [P, H, CT])
        kT, vT = sb("kT", [P, CB, SP_]), sb("vT", [P, CB, SP_])
        v_diag = sb("v_diag", [P, CB * NQB, 2, VW])
        v_exp = sb("v_exp", [P, NC, CB * NQB, 2, VW])
        sT = sb("sT", [P, 2, CT])
        smax = sb("smax", [P, 16])
        probs, pT = sb("probs", [P, 2, CT]), sb("pT", [P, 2, CT])
        rden = sb("rden", [P, 16])
        att = sb("att", [P, 2 * D])
        half = sb("half", [P, S])
        aT = sb("aT", [P, CT])
        at_hi, at_lo = sb("at_hi", [P, CT], f32r), sb("at_lo", [P, CT], f32r)
        oT = sb("oT", [P, CT])
        x1, acc = sb("x1", [P, CB, D]), sb("acc", [P, CB, D])
        x2_hi, x2_lo = sb("x2_hi", [P, CT], f32r), sb("x2_lo", [P, CT], f32r)
        lgT = sb("lgT", [P, CT])
        lg, lgs, lge = sb("lg", [P, CB, E]), sb("lgs", [P, CB, E]), sb("lge", [P, CB, E])
        lmax = sb("lmax", [P, CB])
        gt, eq = sb("gt", [P, CB, E, E]), sb("eq", [P, CB, E, E])
        rank, gsel = sb("rank", [P, CB, E]), sb("gsel", [P, CB, E])
        gsum, gate = sb("gsum", [P, CB]), sb("gate", [P, CB, E])
        h_hi, h_lo = sb("h_hi", [P, HRING, CT], f32r), sb("h_lo", [P, HRING, CT], f32r)
        yT = sb("yT", [P, CT])

        banks = [stack.enter_context(nc.psum_tensor(f"bank{i}", [P, 512], fp32)) for i in range(8)]
        ps_s, ps_t, ps_o, ps_c, h0, h1, y0, y1 = banks
        ps_h = [h0, h1]
        ps_y = [y0, y1]

        ld_consts, ld_wa, ld_x0, ld_x, ld_ctx, ld_w1, ld_w2 = (
            sem(n) for n in ("ld_consts", "ld_wa", "ld_x0", "ld_x", "ld_ctx", "ld_w1", "ld_w2"))
        zeroed, wa_hi_ready, w1_hi_ready, w2_hi_ready = (
            sem(n) for n in ("zeroed", "wa_hi_ready", "w1_hi_ready", "w2_hi_ready"))
        wa_split, w1_split, w2_split = (sem(n) for n in ("wa_split", "w1_split", "w2_split"))
        gelu_b1_ready, d_psum, kappa_ready = (sem(n) for n in ("gelu_b1_ready", "d_psum", "kappa_ready"))
        setup_chain, ln1_chain, ln2_chain, max_chain, den_chain, gate_chain = (
            sem(n) for n in ("setup_chain", "ln1_chain", "ln2_chain", "max_chain", "den_chain", "gate_chain"))
        var1_ready, rstd1_ready, xn1_ready, xT1_psum, xhi1_ready, xlo1_ready = (
            sem(n) for n in ("var1_ready", "rstd1_ready", "xn1_ready", "xT1_psum", "xhi1_ready", "xlo1_ready"))
        var2_ready, rstd2_ready, xn2_ready, xT2_psum, xhi2_ready, xlo2_ready = (
            sem(n) for n in ("var2_ready", "rstd2_ready", "xn2_ready", "xT2_psum", "xhi2_ready", "xlo2_ready"))
        chi_ready, clo_ready = sem("chi_ready"), sem("clo_ready")
        q_psum, k_psum, v_psum = (sem(n) for n in ("q_psum", "k_psum", "v_psum"))
        qT_ready, kT_ready, vT_ready = (sem(n) for n in ("qT_ready", "kT_ready", "vT_ready"))
        qexp_loaded, vdiag_ready, vexp_loaded = (sem(n) for n in ("qexp_loaded", "vdiag_ready", "vexp_loaded"))
        s_psum, sT_ready, sc_psum, shifted_ready = (sem(n) for n in ("s_psum", "sT_ready", "sc_psum", "shifted_ready"))
        p_ready, pT_ready, o_psum, att_ready = (sem(n) for n in ("p_ready", "pT_ready", "o_psum", "att_ready"))
        at_psum, half_ready, aT_ready = (sem(n) for n in ("at_psum", "half_ready", "aT_ready"))
        ahi_ready, alo_ready, proj_psum, oT_ready, back_psum, x1_ready = (
            sem(n) for n in ("ahi_ready", "alo_ready", "proj_psum", "oT_ready", "back_psum", "x1_ready"))
        lgT_psum, lgT_ready, lg_psum, lgs_ready, lge_ready, gate_ready = (
            sem(n) for n in ("lgT_psum", "lgT_ready", "lg_psum", "lgs_ready", "lge_ready", "gate_ready"))
        h_psum, h_ready, hhi_ready, hlo_ready, h_used = (
            sem(n) for n in ("h_psum", "h_ready", "hhi_ready", "hlo_ready", "h_used"))
        yT_ready, yt_psum, y_added, acc_free, out_stored = (
            sem(n) for n in ("yT_ready", "yt_psum", "y_added", "acc_free", "out_stored"))

        block = stack.enter_context(nc.Block())

        def reached(engine, signal, value):
            if not isinstance(value, int) or value > 0:
                engine.wait_ge(signal, value)


        @block.sync
        def _(sp):
            sp.dma_start(x_all[:, 0:CB, :], x[0:CB, :, :].rearrange("b s d -> s b d")).then_inc(ld_x0, 16)
            sp.dma_start(cst[:, :], consts).then_inc(ld_consts, 16)
            sp.dma_start(cols[:, :], pcols).then_inc(ld_consts, 16)
            sp.dma_start(wr_raw[:, :], wr).then_inc(ld_consts, 16)
            sp.dma_start(ctx[:, :], ctxT[:, 0:CT]).then_inc(ld_ctx, 16)
            sp.dma_start(x_all[:, CB:B, :], x[CB:B, :, :].rearrange("b s d -> s b d")).then_inc(ld_x, 16)
            sp.dma_start(w2_raw[:, :], w2).then_inc(ld_w2, 16)
            sp.wait_ge(zeroed, 1)

            def expand_queries(nth):
                sp.wait_ge(qT_ready, nth)
                for h in range(H):
                    sp.dma_start(q_exp[HD * h:HD * (h + 1), h, :], qT[HD * h:HD * (h + 1), :]).then_inc(qexp_loaded, 16)

            def expand_values(nth):
                sp.wait_ge(vdiag_ready, nth)
                for q in range(NC):
                    sp.dma_start(v_exp[32 * q:32 * (q + 1), q, :, :, :],
                                 v_diag[32 * q:32 * (q + 1), :, :, :]).then_inc(vexp_loaded, 16)

            def load_context(split, first_token):
                sp.wait_ge(clo_ready, split)
                sp.dma_start(ctx[:, :], ctxT[:, bass.ds(first_token, CT)]).then_inc(ld_ctx, 16)

            def store(experts, first_batch):
                sp.wait_ge(y_added, experts)
                sp.dma_start(out[bass.ds(first_batch, CB), :, :].rearrange("b s d -> s b d"),
                             acc[:, :, :]).then_inc(out_stored, 16)

            def body(c, ffn=True, proj=True):
                if proj:
                    load_context(c + 1, c * CT + CT)
                    expand_queries(c + 2)
                    expand_values(c + 2)
                if ffn:
                    store(c * E + E, c * CB - CB)

            sp.sem_inc(out_stored, 16)
            sp.sem_inc(y_added, E)
            expand_queries(1)
            expand_values(1)
            body(0, ffn=False)
            with sp.Fori(1, CHUNKS - 1) as c:
                body(c)
            body(CHUNKS - 1, proj=False)
            store(CHUNKS * E + E, (CHUNKS - 1) * CB)
            sp.wait_ge(out_stored, (CHUNKS + 1) * 16)

        @block.gpsimd
        def _(pool):
            nc.gpsimd.memset(neg_half[:, :], -0.5).then_inc(zeroed, 1)
            nc.gpsimd.memset(kT[:, :, 0:QB], 0.0)
            nc.gpsimd.memset(vT[:, :, 0:QB], 0.0)
            nc.gpsimd.memset(v_diag[:, :, :, :], 1.0)
            nc.gpsimd.memset(q_exp[:, :, :], 0.0)
            nc.gpsimd.memset(lgT[:, :], 0.0)
            nc.gpsimd.memset(v_exp[:, :, :, :, :], 0.0).then_inc(zeroed, 1)

            def inverse_deviation(n, var_ready, rstd_ready, veps, rstd):
                pool.wait_ge(var_ready, n + 1)
                nc.gpsimd.tensor_tensor(rstd[:, :], veps[:, :], neg_half[:, :], ALU.pow).then_inc(rstd_ready, 1)

            def context_rest(n):
                pool.wait_ge(chi_ready, n + 1)
                reached(pool, k_psum, n)
                reached(pool, v_psum, n)
                nc.gpsimd.tensor_tensor(ct_lo[:, :], ctx[:, :], ct_hi[:, :].bitcast(fp32), ALU.subtract).then_inc(clo_ready, 1)

            ln1 = (var1_ready, rstd1_ready, veps1, rstd1)
            ln2 = (var2_ready, rstd2_ready, veps2, rstd2)
            pool.wait_ge(zeroed, 2)
            inverse_deviation(0, *ln1)
            context_rest(0)

            def body(c, proj=True):
                if proj:
                    inverse_deviation(c + 1, *ln1)
                    context_rest(c + 1)
                inverse_deviation(c, *ln2)

            body(0)
            with pool.Fori(1, CHUNKS - 1) as c:
                body(c)
            body(CHUNKS - 1, proj=False)

        @block.scalar
        def _(act):
            Id = ACT.Identity
            act.dma_start(wa[:, :, :], wqkvo).then_inc(ld_wa, 16)
            act.dma_start(w1_raw[:, :], w1).then_inc(ld_w1, 16)

            def split_x(n, xT_psum, bank, hi, xhi_ready):
                act.wait_ge(xT_psum, n + 1)
                nc.scalar.activation(hi[:, :], bank[:, :], ACT.Copy).then_inc(xhi_ready, 1)

            def context_rounded(n):
                act.wait_ge(ld_ctx, n * 16 + 16)
                reached(act, v_psum, n)
                nc.scalar.activation(ct_hi[:, :], ctx[:, :], ACT.Copy).then_inc(chi_ready, 1)

            def queries(n):
                act.wait_ge(q_psum, n + 1)
                reached(act, qexp_loaded, n * 16 * H)
                reached(act, s_psum, n * CB)
                nc.scalar.activation(qT[:, :], ps_c[:, :], Id, bias=bq).then_inc(qT_ready, 1)

            def keys(n):
                act.wait_ge(k_psum, n + 1)
                nc.scalar.activation(kT[:, :, QB:SP_], ps_s[:, :].rearrange("p (b s) -> p b s", b=CB), Id,
                                     bias=bk).then_inc(kT_ready, 1)

            def values(n):
                act.wait_ge(v_psum, n + 1)
                reached(act, vdiag_ready, n)
                nc.scalar.activation(vT[:, :, QB:SP_], ps_o[:, :].rearrange("p (b s) -> p b s", b=CB), Id,
                                     bias=bv).then_inc(vT_ready, 1)

            def scores_out(c, b):
                n = c * CB + b
                act.wait_ge(s_psum, n + 1)
                reached(act, sc_psum, n - 1)
                nc.scalar.activation(sT[:, b % 2, :], ps_s[:, :], ACT.Copy).then_inc(sT_ready, 1)

            def exponent(c, b):
                n = c * CB + b
                act.wait_ge(shifted_ready, n + 1)
                nc.scalar.activation(probs[:, b % 2, :], probs[:, b % 2, :], ACT.Exp, scale=float(HD) ** -0.5).then_inc(p_ready, 1)

            def first_half(n):
                act.wait_ge(at_psum, n + 1)
                reached(act, aT_ready, n)
                nc.scalar.activation(half[:, :].rearrange("p (g q) -> p g q", q=QB),
                                     ps_c[:, 0:2 * S].rearrange("p (g i q) -> p g i q", i=2, q=QB)[:, :, 0, :],
                                     ACT.Copy, scale=first_head).then_inc(half_ready, 1)

            def attention_rounded(c):
                act.wait_ge(aT_ready, c * CB + CB)
                nc.scalar.activation(at_hi[:, :], aT[:, :], ACT.Copy).then_inc(ahi_ready, 1)

            def projection_out(c):
                act.wait_ge(proj_psum, c + 1)
                nc.scalar.activation(oT[:, :], ps_o[:, :], Id, bias=bo).then_inc(oT_ready, 1)

            def logits_out(f):
                act.wait_ge(lgT_psum, f + 1)
                nc.scalar.activation(lgT[0:E, :], ps_c[0:E, :], Id, bias=brc).then_inc(lgT_ready, 1)

            def gate_exponent(f):
                act.wait_ge(lgs_ready, f + 1)
                nc.scalar.activation(lge[:, :, :], lgs[:, :, :], ACT.Exp).then_inc(lge_ready, 1)

            def hidden(f, k):
                act.wait_ge(h_psum, f * NK + k + 1)
                if k >= FRING:
                    act.wait_ge(hlo_ready, f * NK + k + 1 - FRING)
                nc.scalar.activation(h_f[:, k % FRING, :], ps_h[k % 2][:, :], ACT.Gelu,
                                     bias=b1c[:, k:k + 1]).then_inc(h_ready, 1)

            def hidden_rounded(f, k):
                act.wait_ge(h_ready, f * NK + k + 1)
                if k >= HRING:
                    act.wait_ge(h_used, f * NK + k + 1 - HRING)
                nc.scalar.activation(h_hi[:, k % HRING, :], h_f[:, k % FRING, :], ACT.Copy).then_inc(hhi_ready, 1)

            def expert_out(f, e):
                act.wait_ge(h_used, f * NK + (e + 1) * HC)
                if e > 0:
                    act.wait_ge(yt_psum, f * E + e)
                nc.scalar.activation(yT[:, :], ps_y[e % 2][:, :], Id, bias=kappa[:, e:e + 1]).then_inc(yT_ready, 1)

            def weights_first():
                act.wait_ge(ld_wa, 16)
                nc.scalar.activation(wa_hi[:, :, :], wa[:, :, :], ACT.Copy)
                act.wait_ge(ld_consts, 48)
                nc.scalar.activation(wr_hi[:, :], wr_raw[:, :], ACT.Copy)
                nc.scalar.activation(mask_l[:, :], cst[0:KW, 146:274], ACT.Copy)
                nc.scalar.activation(mask_r[:, :], cst[0:KW, 274:786], ACT.Copy).then_inc(wa_hi_ready, 1)

            def weights_then():
                act.wait_ge(ld_w1, 16)
                nc.scalar.activation(w1_hi[:, :, :].rearrange("p k m -> p (k m)"), w1_raw[:, :], ACT.Copy).then_inc(w1_hi_ready, 1)
                act.wait_ge(ld_w2, 16)
                nc.scalar.activation(w2_hi[:, :, :].rearrange("p k m -> p (k m)"), w2_raw[:, :], ACT.Copy).then_inc(w2_hi_ready, 1)

            def body(c, ffn=True, proj=True):
                f, n = c - 1, c * CB

                def gelu(*ks):
                    for k in ks if ffn else ():
                        hidden(f, k)

                def rounded(*ks):
                    for k in ks if ffn else ():
                        hidden_rounded(f, k)

                def y_out(*es):
                    for e in es if ffn else ():
                        expert_out(f, e)

                gelu(0, 1)
                rounded(0)
                if ffn:
                    logits_out(f)
                rounded(1)
                scores_out(c, 0)
                gelu(2)
                rounded(2)
                gelu(3)
                rounded(3)
                scores_out(c, 1)
                gelu(4)
                exponent(c, 0)
                scores_out(c, 2)
                exponent(c, 1)
                gelu(5, 6)
                rounded(4)
                scores_out(c, 3)
                first_half(n + 0)
                if proj:
                    context_rounded(c + 1)
                gelu(7)
                exponent(c, 2)
                first_half(n + 1)
                rounded(5)
                if ffn:
                    gate_exponent(f)
                rounded(6)
                exponent(c, 3)
                if proj:
                    split_x(c + 1, xT1_psum, ps_c, xt_hi, xhi1_ready)
                rounded(7)
                gelu(8)
                if proj:
                    queries(c + 1)
                y_out(0)
                if proj:
                    keys(c + 1)
                first_half(n + 2)
                gelu(9)
                rounded(8)
                gelu(10)
                first_half(n + 3)
                rounded(9)
                attention_rounded(c)
                y_out(1)
                rounded(10)
                gelu(11)
                rounded(11)
                projection_out(c)
                gelu(12)
                rounded(12)
                gelu(13, 14)
                rounded(13, 14)
                gelu(15)
                y_out(2)
                rounded(15)
                split_x(c, xT2_psum, ps_t, x2_hi, xhi2_ready)
                y_out(3)
                if proj:
                    values(c + 1)

            def last_experts(f):
                def gelu(*ks):
                    for k in ks:
                        hidden(f, k)

                def rounded(*ks):
                    for k in ks:
                        hidden_rounded(f, k)

                def y_out(*es):
                    for e in es:
                        expert_out(f, e)

                gelu(0, 1)
                rounded(0)
                gelu(2)
                rounded(1)
                gelu(3)
                rounded(2)
                gelu(4)
                rounded(3)
                gelu(5)
                logits_out(f)
                rounded(4)
                gelu(6)
                rounded(5)
                gelu(7)
                rounded(6)
                y_out(0)
                gelu(8)
                rounded(7)
                gelu(9)
                rounded(8)
                gate_exponent(f)
                gelu(10)
                rounded(9)
                gelu(11)
                rounded(10)
                gelu(12)
                y_out(1)
                rounded(11)
                gelu(13)
                rounded(12)
                gelu(14)
                rounded(13, 14)
                gelu(15)
                rounded(15)
                y_out(2, 3)

            weights_first()
            nc.scalar.activation(gelu_b1[:, :], b1c, ACT.Gelu).then_inc(gelu_b1_ready, 1)
            act.wait_ge(zeroed, 2)
            split_x(0, xT1_psum, ps_c, xt_hi, xhi1_ready)
            context_rounded(0)
            queries(0)
            keys(0)
            values(0)
            weights_then()
            body(0, ffn=False)
            act.wait_ge(kappa_ready, 1)
            with act.Fori(1, CHUNKS - 1) as c:
                body(c)
            body(CHUNKS - 1, proj=False)
            last_experts(CHUNKS - 1)

        @block.vector
        def _(dve):
            V = nc.vector

            def link(ins, chain, value):
                ins.then_inc(chain, 1)
                dve.wait_ge(chain, value)

            def weights_first():
                dve.wait_ge(wa_hi_ready, 1)
                V.tensor_tensor(wa_lo[:, :, :], wa[:, :, :], wa_hi[:, :, :].bitcast(fp32), ALU.subtract)
                V.tensor_tensor(wr_lo[:, :], wr_raw[:, :], wr_hi[:, :].bitcast(fp32), ALU.subtract).then_inc(wa_split, 1)

            def weights_then():
                dve.wait_ge(w1_hi_ready, 1)
                V.tensor_tensor(w1_lo[:, :, :].rearrange("p k m -> p (k m)"), w1_raw[:, :],
                                w1_hi[:, :, :].rearrange("p k m -> p (k m)").bitcast(fp32), ALU.subtract).then_inc(w1_split, 1)
                dve.wait_ge(w2_hi_ready, 1)
                V.tensor_tensor(w2_lo[:, :, :].rearrange("p k m -> p (k m)"), w2_raw[:, :],
                                w2_hi[:, :, :].rearrange("p k m -> p (k m)").bitcast(fp32), ALU.subtract).then_inc(w2_split, 1)

            def constants_of_experts():
                dve.wait_ge(d_psum, 1)
                V.tensor_reduce(csum[:, 0:1], y0[:, 0:E], X, ALU.add)
                link(V.tensor_reduce(csum[:, 1:2], b2c, X, ALU.add), setup_chain, 1)
                link(V.tensor_tensor(csum[:, 0:1], csum[:, 0:1], csum[:, 1:2], ALU.add), setup_chain, 2)
                V.tensor_scalar(kappa[:, :], y0[:, 0:E], -1.0, csum[:, 0:1], ALU.mult, ALU.add).then_inc(kappa_ready, 1)

            def statistics(n, src, chain, var_ready, mv, veps):
                for b in range(CB):
                    last = V.bn_stats(stats[:, b, :], src[b])
                link(last, chain, n * 2 + 1)
                V.memset(fence[:, 0:1], 0.0)
                for b in range(CB):
                    last = V.bn_aggr(mv[:, b, :], stats[:, b, :])
                link(last, chain, n * 2 + 2)
                V.tensor_scalar(veps[:, :], mv[:, :, 1], EPS, None, ALU.add).then_inc(var_ready, 1)

            def normalized(n, src, rstd_ready, xT_psum, mv, rstd, xn, xn_ready):
                dve.wait_ge(rstd_ready, n + 1)
                reached(dve, xT_psum, n)
                for b in range(CB):
                    last = V.tensor_scalar(xn[:, b, :], src[b], mv[:, b, 0:1], rstd[:, b:b + 1],
                                           ALU.subtract, ALU.mult)
                last.then_inc(xn_ready, 1)

            def x_tiles(n):
                return [x_all[:, bass.ds(n * CB + b, 1), :].rearrange("p o d -> p (o d)") for b in range(CB)]

            def statistics1(n):
                statistics(n, x_tiles(n), ln1_chain, var1_ready, mv1, veps1)

            def normalized1(n):
                normalized(n, x_tiles(n), rstd1_ready, xT1_psum, mv1, rstd1, xn1, xn1_ready)

            def windows(t, b):
                a = t[:, b, 0:KW]
                return bass.AP(a.tensor, a.offset, [list(a.ap[0]), [QB, NQB], [1, KW]])

            def values_in(n):
                dve.wait_ge(vT_ready, n + 1)
                reached(dve, vexp_loaded, n * 16 * NC)
                reached(dve, o_psum, n * CB)
                for b in range(CB):
                    last = V.transpose(v_diag[:, b * NQB:(b + 1) * NQB, :, 0:2 * HD], windows(vT, b))
                last.then_inc(vdiag_ready, 1)

            def split_lo(n, bank, hi, lo, xhi_ready, xlo_ready):
                dve.wait_ge(xhi_ready, n + 1)
                V.tensor_tensor(lo[:, :], bank[:, :], hi[:, :].bitcast(fp32), ALU.subtract).then_inc(xlo_ready, 1)

            x1_tiles = [x1[:, b, :] for b in range(CB)]

            def shift(c, b):
                n = c * CB + b
                dve.wait_ge(sc_psum, n + 1)
                blocks = ps_t[:, :].rearrange("p (g k) -> p g k", k=KW)
                link(V.tensor_reduce(smax[:, :], blocks, X, ALU.max), max_chain, n + 1)
                reached(dve, pT_ready, n - 1)
                V.tensor_tensor(probs[:, b % 2, :].rearrange("p (g k) -> p g k", k=KW), blocks,
                                smax[:, :, None].to_broadcast([P, 16, KW]), ALU.subtract).then_inc(shifted_ready, 1)

            def keys_first(c, b):
                n = c * CB + b
                dve.wait_ge(p_ready, n + 1)
                reached(dve, o_psum, n - 1)
                V.transpose(pT[:, b % 2, :], probs[:, b % 2, :]).then_inc(pT_ready, 1)

            def normalize(n):
                dve.wait_ge(o_psum, n + 1)
                o = ps_o[:, 0:16 * VW].rearrange("p (g v) -> p g v", v=VW)
                link(V.reciprocal(rden[:, :], o[:, :, 2 * HD]), den_chain, n + 1)
                reached(dve, at_psum, n)
                V.tensor_tensor(att[:, :].rearrange("p (g v) -> p g v", v=2 * HD), o[:, :, 0:2 * HD],
                                rden[:, :, None].to_broadcast([P, 16, 2 * HD]), ALU.mult).then_inc(att_ready, 1)

            def second_half(c, b):
                n = c * CB + b
                dve.wait_ge(half_ready, n + 1)
                reached(dve, alo_ready, c)
                V.scalar_tensor_tensor(aT[:, b * S:(b + 1) * S].rearrange("p (g q) -> p g q", q=QB),
                                       ps_c[:, 0:2 * S].rearrange("p (g i q) -> p g i q", i=2, q=QB)[:, :, 1, :],
                                       second_head, half[:, :].rearrange("p (g q) -> p g q", q=QB),
                                       ALU.mult, ALU.add).then_inc(aT_ready, 1)

            def attention_rest(c):
                dve.wait_ge(ahi_ready, c + 1)
                V.tensor_tensor(at_lo[:, :], aT[:, :], at_hi[:, :].bitcast(fp32), ALU.subtract).then_inc(alo_ready, 1)

            def residual(c, ffn):
                dve.wait_ge(back_psum, c + 1)
                if ffn:
                    dve.wait_ge(y_added, c * E + 1)
                V.tensor_tensor(x1[:, :, :], ps_t[:, :].rearrange("p (b d) -> p b d", b=CB),
                                x_all[:, bass.ds(c * CB, CB), :], ALU.add).then_inc(x1_ready, 1)
                dve.wait_ge(x1_ready, c + 1)

            def gate_logits(f):
                dve.wait_ge(lg_psum, f + 1)
                link(V.tensor_copy(lg[:, :, :], ps_c[:, :].rearrange("p (b e) -> p b e", b=CB)[:, :, 0:E]),
                     gate_chain, f * 9 + 1)
                link(V.tensor_reduce(lmax[:, :], lg[:, :, :], X, ALU.max), gate_chain, f * 9 + 2)
                V.tensor_tensor(lgs[:, :, :], lg[:, :, :], lmax[:, :, None].to_broadcast([P, CB, E]),
                                ALU.subtract).then_inc(lgs_ready, 1)

            def gate_ranks(f):
                others = lg[:, :, None, :].to_broadcast([P, CB, E, E])
                own = lg[:, :, :, None].to_broadcast([P, CB, E, E])
                V.tensor_tensor(gt[:, :, :, :], others, own, ALU.is_gt)
                link(V.tensor_tensor(eq[:, :, :, :], others, own, ALU.is_equal), gate_chain, f * 9 + 3)
                link(V.tensor_tensor(eq[:, :, :, :], eq[:, :, :, :], lower[:, None, :, :].to_broadcast([P, CB, E, E]),
                                     ALU.mult), gate_chain, f * 9 + 4)
                link(V.tensor_tensor(gt[:, :, :, :], gt[:, :, :, :], eq[:, :, :, :], ALU.add), gate_chain, f * 9 + 5)
                link(V.tensor_reduce(rank[:, :, :], gt[:, :, :, :], X, ALU.add), gate_chain, f * 9 + 6)

            def gate_weights(f):
                dve.wait_ge(lge_ready, f + 1)
                link(V.scalar_tensor_tensor(gsel[:, :, :], rank[:, :, :], 2.0, lge[:, :, :], ALU.is_lt, ALU.mult),
                     gate_chain, f * 9 + 7)
                link(V.tensor_reduce(gsum[:, :], gsel[:, :, :], X, ALU.add), gate_chain, f * 9 + 8)
                link(V.reciprocal(gsum[:, :], gsum[:, :]), gate_chain, f * 9 + 9)
                V.tensor_tensor(gate[:, :, :], gsel[:, :, :], gsum[:, :, None].to_broadcast([P, CB, E]),
                                ALU.mult).then_inc(gate_ready, 1)

            def hidden_lo(f, k):
                dve.wait_ge(hhi_ready, f * NK + k + 1)
                V.tensor_tensor(h_lo[:, k % HRING, :], h_f[:, k % FRING, :], h_hi[:, k % HRING, :].bitcast(fp32),
                                ALU.subtract).then_inc(hlo_ready, 1)

            def add_expert(f, e):
                dve.wait_ge(yt_psum, f * E + e + 1)
                if e == 0:
                    dve.wait_ge(gate_ready, f + 1)
                    dve.wait_ge(out_stored, f * 16 + 16)
                else:
                    dve.wait_ge(y_added, f * E + E + e)
                before = x1 if e == 0 else acc
                for b in range(CB):
                    last = V.scalar_tensor_tensor(acc[:, b, :], ps_s[:, b * S:(b + 1) * S], gate[:, b, e:e + 1],
                                                  before[:, b, :], ALU.mult, ALU.add)
                last.then_inc(y_added, 1)

            def body(c, ffn=True, proj=True):
                f, n = c - 1, c * CB

                def lo(*ks):
                    for k in ks if ffn else ():
                        hidden_lo(f, k)

                def add(*es):
                    for e in es if ffn else ():
                        add_expert(f, e)

                if proj:
                    statistics1(c + 1)
                lo(0)
                shift(c, 0)
                if proj:
                    normalized1(c + 1)
                lo(1)
                shift(c, 1)
                keys_first(c, 0)
                lo(2)
                keys_first(c, 1)
                if ffn:
                    gate_logits(f)
                lo(3)
                normalize(n + 0)
                shift(c, 2)
                lo(4)
                second_half(c, 0)
                normalize(n + 1)
                shift(c, 3)
                second_half(c, 1)
                keys_first(c, 2)
                if ffn:
                    gate_ranks(f)
                keys_first(c, 3)
                if proj:
                    split_lo(c + 1, ps_c, xt_hi, xt_lo, xhi1_ready, xlo1_ready)
                normalize(n + 2)
                lo(5)
                if ffn:
                    gate_weights(f)
                lo(6)
                normalize(n + 3)
                second_half(c, 2)
                lo(7, 8)
                second_half(c, 3)
                add(0)
                attention_rest(c)
                lo(9, 10)
                add(1)
                lo(11)
                residual(c, ffn)
                lo(12)
                statistics(c, x1_tiles, ln2_chain, var2_ready, mv2, veps2)
                lo(13, 14)
                normalized(c, x1_tiles, rstd2_ready, xT2_psum, mv2, rstd2, xn2, xn2_ready)
                lo(15)
                add(2)
                split_lo(c, ps_t, x2_hi, x2_lo, xhi2_ready, xlo2_ready)
                add(3)
                if proj:
                    values_in(c + 1)

            def last_experts(f):
                def lo(*ks):
                    for k in ks:
                        hidden_lo(f, k)

                def add(*es):
                    for e in es:
                        add_expert(f, e)

                lo(0, 1, 2, 3, 4, 5, 6)
                gate_logits(f)
                lo(7)
                gate_ranks(f)
                gate_weights(f)
                lo(8, 9)
                add(0)
                lo(10, 11)
                add(1)
                lo(12, 13, 14, 15)
                add(2, 3)

            dve.wait_ge(ld_x0, 16)
            statistics1(0)
            normalized1(0)
            weights_first()
            split_lo(0, ps_c, xt_hi, xt_lo, xhi1_ready, xlo1_ready)
            values_in(0)
            weights_then()
            constants_of_experts()
            dve.wait_ge(ld_x, 16)
            body(0, ffn=False)
            with dve.Fori(1, CHUNKS - 1) as c:
                body(c)
            body(CHUNKS - 1, proj=False)
            last_experts(CHUNKS - 1)

        @block.tensor
        def _(pe):
            mm = nc.tensor.matmul

            def split_mm(ps, w_hi, w_lo, r_hi, r_lo, start=True, stop=True):
                mm(ps, w_hi, r_hi, start=start, stop=False)
                mm(ps, w_hi, r_lo, start=False, stop=False)
                return mm(ps, w_lo, r_hi, start=False, stop=stop)

            def transposes(bank, src):
                for b in range(CB):
                    last = nc.tensor.transpose(bank[:, b * P:(b + 1) * P], src(b), ident)
                return last

            def constants_of_experts():
                pe.wait_ge(gelu_b1_ready, 1)
                pe.wait_ge(ld_w2, 16)
                for e in range(E):
                    for k in range(HC):
                        i = e * HC + k
                        last = mm(y0[:, e:e + 1], w2_raw[:, i * P:(i + 1) * P], gelu_b1[:, i:i + 1],
                                  start=(k == 0), stop=(k == HC - 1))
                last.then_inc(d_psum, 1)


            def input_columns(n):
                pe.wait_ge(xn1_ready, n + 1)
                reached(pe, aT_ready, n * CB - CB + 2)
                transposes(ps_c, lambda b: xn1[:, b, :]).then_inc(xT1_psum, 1)

            def queries(n):
                pe.wait_ge(xlo1_ready, n + 1)
                split_mm(ps_c[:, :], wa_hi[:, 0, :], wa_lo[:, 0, :], xt_hi[:, :], xt_lo[:, :]).then_inc(q_psum, 1)

            def keys(n):
                pe.wait_ge(clo_ready, n + 1)
                reached(pe, sT_ready, n * CB)
                split_mm(ps_s[:, :], wa_hi[:, 1, :], wa_lo[:, 1, :], ct_hi[:, :], ct_lo[:, :]).then_inc(k_psum, 1)

            def values(n):
                pe.wait_ge(clo_ready, n + 1)
                reached(pe, oT_ready, n)
                split_mm(ps_o[:, :], wa_hi[:, 2, :], wa_lo[:, 2, :], ct_hi[:, :], ct_lo[:, :]).then_inc(v_psum, 1)

            def scores(c, b, ffn):
                n = c * CB + b
                if b == 0:
                    pe.wait_ge(kT_ready, c + 1)
                    pe.wait_ge(qexp_loaded, (c + 1) * 16 * H)
                    if ffn:
                        pe.wait_ge(y_added, c * E)
                else:
                    pe.wait_ge(sT_ready, n)
                mm(ps_s[:, :], mask_l[:, :], mask_r[:, :], start=True, stop=False, skip_group_check=True)
                for quad in range(QUADS):
                    for j in range(4):
                        t = QB * (4 * quad + j)
                        last = mm(ps_s[32 * j:32 * (j + 1), quad * 256:(quad + 1) * 256], kT[:, b, t:t + KW],
                                  q_exp[:, :, b * S + t:b * S + t + QB], start=False, stop=True,
                                  skip_group_check=True)
                last.then_inc(s_psum, 1)

            def score_rows(c, b):
                n = c * CB + b
                pe.wait_ge(sT_ready, n + 1)
                if b > 0:
                    pe.wait_ge(shifted_ready, n)
                transposes(ps_t, lambda i: sT[:, b % 2, i * P:(i + 1) * P]).then_inc(sc_psum, 1)

            def attend(c, b):
                n = c * CB + b
                if b == 0:
                    pe.wait_ge(vexp_loaded, (c + 1) * 16 * NC)
                pe.wait_ge(pT_ready, n + 1)
                reached(pe, att_ready, n)
                for quad in range(QUADS):
                    for g in range(2):
                        for j in range(4):
                            i = quad * 2 + g
                            last = mm(ps_o[32 * j:32 * (j + 1), i * NC * VW:(i + 1) * NC * VW],
                                      pT[:, b % 2, (4 * i + j) * KW:(4 * i + j + 1) * KW],
                                      v_exp[:, :, b * NQB + 4 * quad + j, g, :], start=True, stop=True,
                                      skip_group_check=True)
                last.then_inc(o_psum, 1)

            def attention_columns(c, b, ffn, proj):
                n = c * CB + b
                pe.wait_ge(att_ready, n + 1)
                if b == 0 and ffn:
                    pe.wait_ge(lgs_ready, c)
                elif b == 2 and proj:
                    pe.wait_ge(qT_ready, c + 2)
                elif b > 0:
                    pe.wait_ge(aT_ready, n)
                for quad in range(QUADS):
                    last = nc.tensor.transpose(ps_c[:, quad * P:(quad + 1) * P], att[:, quad * P:(quad + 1) * P], ident)
                last.then_inc(at_psum, 1)

            def projection(c):
                pe.wait_ge(alo_ready, c + 1)
                split_mm(ps_o[:, :], wa_hi[:, 3, :], wa_lo[:, 3, :], at_hi[:, :], at_lo[:, :]).then_inc(proj_psum, 1)

            def back(c):
                pe.wait_ge(oT_ready, c + 1)
                transposes(ps_t, lambda b: oT[:, b * P:(b + 1) * P]).then_inc(back_psum, 1)

            def normalized_columns(c):
                pe.wait_ge(xn2_ready, c + 1)
                transposes(ps_t, lambda b: xn2[:, b, :]).then_inc(xT2_psum, 1)

            def logits(f):
                pe.wait_ge(xlo2_ready, f + 1)
                split_mm(ps_c[0:E, :], wr_hi[:, :], wr_lo[:, :], x2_hi[:, :], x2_lo[:, :]).then_inc(lgT_psum, 1)

            def logit_rows(f):
                pe.wait_ge(lgT_ready, f + 1)
                transposes(ps_c, lambda b: lgT[:, b * P:(b + 1) * P]).then_inc(lg_psum, 1)

            def first_layer(f, k):
                if k == 0:
                    pe.wait_ge(xlo2_ready, f + 1)
                if k >= 2:
                    pe.wait_ge(h_ready, f * NK + k - 1)
                split_mm(ps_h[k % 2][:, :], w1_hi[:, k, :], w1_lo[:, k, :], x2_hi[:, :], x2_lo[:, :]).then_inc(h_psum, 1)

            def second_layer(f, k):
                e = k // HC
                pe.wait_ge(hlo_ready, f * NK + k + 1)
                r = k % HRING
                split_mm(ps_y[e % 2][:, :], w2_hi[:, k, :], w2_lo[:, k, :], h_hi[:, r, :], h_lo[:, r, :],
                         start=(k % HC == 0), stop=(k % HC == HC - 1)).then_inc(h_used, 1)

            def expert_rows(f, e, proj):
                pe.wait_ge(yT_ready, f * E + e + 1)
                if e == 0 and proj:
                    pe.wait_ge(kT_ready, f + 3)
                pe.wait_ge(y_added, f * E + E + e)
                transposes(ps_s, lambda b: yT[:, b * P:(b + 1) * P]).then_inc(yt_psum, 1)

            def body(c, ffn=True, proj=True):
                f = c - 1

                def l1(*ks):
                    for k in ks if ffn else ():
                        first_layer(f, k)

                def l2(*ks):
                    for k in ks if ffn else ():
                        second_layer(f, k)

                def rows(*es):
                    for e in es if ffn else ():
                        expert_rows(f, e, proj)

                l1(0, 1)
                if ffn:
                    logits(f)
                scores(c, 0, ffn)
                l1(2, 3)
                score_rows(c, 0)
                scores(c, 1, ffn)
                l1(4, 5)
                score_rows(c, 1)
                scores(c, 2, ffn)
                l1(6)
                if ffn:
                    logit_rows(f)
                score_rows(c, 2)
                attend(c, 0)
                scores(c, 3, ffn)
                l1(7)
                attention_columns(c, 0, ffn, proj)
                attend(c, 1)
                l2(0)
                score_rows(c, 3)
                l2(1)
                attention_columns(c, 1, ffn, proj)
                l2(2)
                l1(8, 9)
                if proj:
                    input_columns(c + 1)
                attend(c, 2)
                l2(3)
                if proj:
                    keys(c + 1)
                    queries(c + 1)
                l2(4)
                attend(c, 3)
                attention_columns(c, 2, ffn, proj)
                l1(10)
                l2(5)
                rows(0)
                attention_columns(c, 3, ffn, proj)
                l2(6, 7)
                l1(11, 12)
                rows(1)
                projection(c)
                l1(13)
                l2(8)
                back(c)
                l1(14)
                l2(9, 10)
                l1(15)
                l2(11, 12, 13)
                rows(2)
                l2(14)
                normalized_columns(c)
                l2(15)
                if proj:
                    values(c + 1)
                rows(3)

            def last_experts(f):
                def l1(*ks):
                    for k in ks:
                        first_layer(f, k)

                def l2(*ks):
                    for k in ks:
                        second_layer(f, k)

                def rows(*es):
                    for e in es:
                        expert_rows(f, e, False)

                l1(0, 1, 2, 3)
                logits(f)
                l1(4)
                l2(0)
                l1(5)
                l2(1)
                l1(6, 7)
                l2(2, 3)
                l1(8)
                logit_rows(f)
                l1(9)
                l2(4, 5)
                l1(10)
                l2(6, 7)
                rows(0)
                l1(11)
                l2(8)
                l1(12, 13)
                l2(9)
                l1(14)
                rows(1)
                l2(10, 11)
                l1(15)
                l2(12, 13, 14)
                rows(2)
                l2(15)
                rows(3)

            pe.wait_ge(ld_consts, 48)
            input_columns(0)
            pe.wait_ge(wa_split, 1)
            queries(0)
            keys(0)
            values(0)
            constants_of_experts()
            body(0, ffn=False)
            pe.wait_ge(w1_split, 1)
            pe.wait_ge(w2_split, 1)
            pe.wait_ge(kappa_ready, 1)
            with pe.Fori(1, CHUNKS - 1) as c:
                body(c)
            body(CHUNKS - 1, proj=False)
            last_experts(CHUNKS - 1)


_SHAPES = {"x": (B, S, D), "ctxT": (D, B * S), "wqkvo": (D, 4, D), "w1": (D, NK * P), "w2": (P, NK * D),
           "pcols": (P, 28), "wr": (D, E), "consts": (P, 786)}


def constants():
    import numpy as np
    c = np.zeros((P, 786), np.float32)
    c[:, 0:128] = np.eye(P)
    head = (np.arange(P) // HD) % 2
    c[:, 128] = head == 0
    c[:, 129] = head == 1
    c[:, 130:146] = (np.arange(E)[None, :] < np.arange(E)[:, None]).reshape(1, 16)
    for quad in range(QUADS):
        for q in range(QB):
            for j in range(4):
                for k in range(KW):
                    last = min(q + W, 2 * q + 1) if quad == 0 and j == 0 else q + W
                    if not q + 1 <= k <= last:
                        c[quad * QB + q, 146 + j * KW + k] = -1e30
            c[quad * QB + q, 274 + quad * 256 + q + QB * np.arange(H)] = 1.0
    return c


def kernel(**inputs):
    import numpy as np
    import concourse.bacc as bacc
    from concourse import mybir as mb
    from concourse.bass_utils import run_bass_kernel_spmd

    a = {k: np.ascontiguousarray(v) for k, v in inputs.items()}
    order = np.arange(D).reshape(2, NC, 2, HD).transpose(1, 0, 2, 3).reshape(-1)
    wv, bv = a["L0_xattn_Wv"][order, :], a["L0_xattn_bv"][order]
    br = np.zeros(P, np.float32)
    br[:E] = a["L0_ffn_br"]
    arrays = {
        "x": a["x"],
        "ctxT": a["ctx_1024"].transpose(2, 0, 1).reshape(D, B * S),
        "wqkvo": np.stack([a["L0_xattn_Wq"].T, a["L0_xattn_Wk"].T, wv.T, a["L0_xattn_Wo"].T], axis=1),
        "w1": a["L0_ffn_w1"].reshape(E, D, HC, P).transpose(1, 0, 2, 3).reshape(D, NK * P),
        "w2": a["L0_ffn_w2"].reshape(E, HC, P, D).transpose(2, 0, 1, 3).reshape(P, NK * D),
        "pcols": np.concatenate([
            np.stack([a["L0_xattn_bq"], a["L0_xattn_bk"], bv, a["L0_xattn_bo"]], axis=1),
            a["L0_ffn_b1"].reshape(NK, P).T, a["L0_ffn_b2"].T, br[:, None], np.zeros((P, 3), np.float32)], axis=1),
        "wr": a["L0_ffn_wr"],
        "consts": constants(),
    }
    arrays = {k: np.ascontiguousarray(v) for k, v in arrays.items()}
    nc = bacc.Bacc("TRN2", target_bir_lowering=False, num_devices=1)
    aps = [nc.dram_tensor(f"in_{k}", arrays[k].shape, mb.dt.from_np(arrays[k].dtype), kind="ExternalInput").ap()
           for k in _SHAPES]
    out = nc.dram_tensor("out", (B, S, D), mb.dt.float32, kind="ExternalOutput").ap()
    xattn_ffn_kernel(nc, *aps, out)
    r = run_bass_kernel_spmd(nc, [{f"in_{k}": v for k, v in arrays.items()}], core_ids=[0])
    return r.results[0]["out"]
```

```python
import concourse.bass as bass
from concourse import mybir
from contextlib import ExitStack

B, S, D = 16, 128, 128
H, HD, W = 16, 8, 16
E, F = 4, 512
P = 128
EPS = 1e-5

CB = 4
CT = CB * S
CHUNKS = B // CB
QB = 16
KW = 2 * QB
NQB = S // QB
QUADS = NQB // 4
SP_ = QB + S
NC = 4
VW = 2 * HD + 1
HC = F // P
NK = E * HC
HRING = 8
CONSTS = P + 2 + E * E + QUADS * QB + H
FRING = 4
POOLS = 1


def xattn_ffn_kernel(nc, x, ctxT, wqkvo, w1, w2, pcols, wr, consts, out):
    fp32 = mybir.dt.float32
    f32r = mybir.dt.float32r
    bf16 = mybir.dt.bfloat16
    ALU = mybir.AluOpType
    ACT = mybir.ActivationFunctionType
    X = mybir.AxisListType.X

    with ExitStack() as stack:
        def sb(name, shape, dt=fp32):
            return stack.enter_context(nc.sbuf_tensor(name, shape, dt))

        def sem(name):
            return stack.enter_context(nc.semaphore(name))

        wa = sb("wa", [P, 4, D])
        wa_hi, wa_lo = sb("wa_hi", [P, 4, D], f32r), sb("wa_lo", [P, 4, D], f32r)
        w2_raw = sb("w2_raw", [P, NK * P])
        h_f = sb("h_f", [P, FRING, CT])
        w1_raw = h_f[:, :, :].rearrange("p r t -> p (r t)")
        w1_hi, w1_lo = sb("w1_hi", [P, NK, P], f32r), sb("w1_lo", [P, NK, P], f32r)
        w2_hi, w2_lo = sb("w2_hi", [P, NK, P], f32r), sb("w2_lo", [P, NK, P], f32r)
        cols = sb("cols", [P, 28])
        wr_raw, wr_hi, wr_lo = sb("wr_raw", [P, E]), sb("wr_hi", [P, E], f32r), sb("wr_lo", [P, E], f32r)
        cst = sb("cst", [P, CONSTS])
        ident = cst[:, 0:128]
        first_head, second_head = cst[:, 128:129], cst[:, 129:130]
        lower = cst[:, 130:146].rearrange("p (e j) -> p e j", e=E)
        head_mask = cst[:, 178:178 + H]
        mask = cst[:, 146:178].rearrange("p (u q) -> p u q", u=QUADS)
        bq, bk, bv, bo = (cols[:, i:i + 1] for i in range(4))
        b1c, b2c, brc = cols[:, 4:20], cols[:, 20:24], cols[0:E, 24:25]
        neg_half = sb("neg_half", [P, CB])
        gelu_b1 = sb("gelu_b1", [P, NK])
        csum, kappa = sb("csum", [P, 2]), sb("kappa", [P, E])

        x_all = sb("x_all", [P, B, D])
        ctx = sb("ctx", [P, CT])
        fence = sb("fence", [P, 2])
        stats = sb("stats", [P, CB, 6])
        mv1, veps1, rstd1 = sb("mv1", [P, CB, 2]), sb("veps1", [P, CB]), sb("rstd1", [P, CB])
        mv2, veps2, rstd2 = sb("mv2", [P, CB, 2]), sb("veps2", [P, CB]), sb("rstd2", [P, CB])
        xn1, xn2 = sb("xn1", [P, CB, D]), sb("xn2", [P, CB, D])
        xt_hi, xt_lo = sb("xt_hi", [P, CT], f32r), sb("xt_lo", [P, CT], f32r)
        ct_hi, ct_lo = sb("ct_hi", [P, CT], f32r), sb("ct_lo", [P, CT], f32r)
        qT = sb("qT", [P, CT])
        q_exp = sb("q_exp", [P, H, CT])
        kT, vT = sb("kT", [P, CB, SP_]), sb("vT", [P, CB, SP_])
        v_diag = sb("v_diag", [P, CB * NQB, 2, VW])
        v_exp = sb("v_exp", [P, NC, CB * NQB, 2, VW])
        sT = sb("sT", [P, 2, CT])
        smax = sb("smax", [P, 16])
        probs, pT = sb("probs", [P, 2, CT]), sb("pT", [P, 2, CT])
        rden = sb("rden", [P, 16])
        att = sb("att", [P, 2 * D])
        half = sb("half", [P, S])
        aT = sb("aT", [P, CT])
        at_hi, at_lo = sb("at_hi", [P, CT], f32r), sb("at_lo", [P, CT], f32r)
        oT = sb("oT", [P, CT])
        x1, acc = sb("x1", [P, CB, D]), sb("acc", [P, CB, D])
        idle = acc[:, :, :].rearrange("p b d -> p (b d)").bitcast(bf16)[:, 0:CT]
        x2_hi, x2_lo = sb("x2_hi", [P, CT], f32r), sb("x2_lo", [P, CT], f32r)
        lgT = sb("lgT", [P, CT])
        lg, lgs, lge = sb("lg", [P, CB, E]), sb("lgs", [P, CB, E]), sb("lge", [P, CB, E])
        lmax = sb("lmax", [P, CB])
        gt, eq = sb("gt", [P, CB, E, E]), sb("eq", [P, CB, E, E])
        rank, gsel = sb("rank", [P, CB, E]), sb("gsel", [P, CB, E])
        gsum, gate = sb("gsum", [P, CB]), sb("gate", [P, CB, E])
        h_hi, h_lo = sb("h_hi", [P, HRING, CT], f32r), sb("h_lo", [P, HRING, CT], f32r)
        yT = sb("yT", [P, CT])

        banks = [stack.enter_context(nc.psum_tensor(f"bank{i}", [P, 512], fp32)) for i in range(8)]
        ps_s, ps_t, ps_o, ps_c, h0, h1, y0, y1 = banks
        ps_h = [h0, h1]
        ps_y = [y0, y1]

        ld_consts, ld_wa, ld_x0, ld_x, ld_ctx, ld_w1, ld_w2 = (
            sem(n) for n in ("ld_consts", "ld_wa", "ld_x0", "ld_x", "ld_ctx", "ld_w1", "ld_w2"))
        zeroed, idle_zeroed, v_zeroed, wa_hi_ready, w1_hi_ready, w2_hi_ready = (
            sem(n) for n in ("zeroed", "idle_zeroed", "v_zeroed", "wa_hi_ready", "w1_hi_ready", "w2_hi_ready"))
        wa_split, w1_split, w2_split = (sem(n) for n in ("wa_split", "w1_split", "w2_split"))
        gelu_b1_ready, d_psum, kappa_ready = (sem(n) for n in ("gelu_b1_ready", "d_psum", "kappa_ready"))
        setup_chain, ln1_chain, ln2_chain, max_chain, den_chain, gate_chain = (
            sem(n) for n in ("setup_chain", "ln1_chain", "ln2_chain", "max_chain", "den_chain", "gate_chain"))
        var1_ready, rstd1_ready, xn1_ready, xT1_psum, xhi1_ready, xlo1_ready = (
            sem(n) for n in ("var1_ready", "rstd1_ready", "xn1_ready", "xT1_psum", "xhi1_ready", "xlo1_ready"))
        var2_ready, rstd2_ready, xn2_ready, xT2_psum, xhi2_ready, xlo2_ready = (
            sem(n) for n in ("var2_ready", "rstd2_ready", "xn2_ready", "xT2_psum", "xhi2_ready", "xlo2_ready"))
        chi_ready, clo_ready = sem("chi_ready"), sem("clo_ready")
        q_psum, k_psum, v_psum = (sem(n) for n in ("q_psum", "k_psum", "v_psum"))
        qT_ready, kT_ready, vT_ready = (sem(n) for n in ("qT_ready", "kT_ready", "vT_ready"))
        q_masked_dve, q_masked_pool = sem("q_masked_dve"), sem("q_masked_pool")
        qexp_loaded, vdiag_ready, vexp_loaded = (sem(n) for n in ("qexp_loaded", "vdiag_ready", "vexp_loaded"))
        s_psum, sT_ready, sc_psum, shifted_ready = (sem(n) for n in ("s_psum", "sT_ready", "sc_psum", "shifted_ready"))
        p_ready, pT_ready, o_psum, att_ready = (sem(n) for n in ("p_ready", "pT_ready", "o_psum", "att_ready"))
        at_psum, half_ready, aT_ready = (sem(n) for n in ("at_psum", "half_ready", "aT_ready"))
        ahi_ready, alo_ready, proj_psum, oT_ready, back_psum, x1_ready = (
            sem(n) for n in ("ahi_ready", "alo_ready", "proj_psum", "oT_ready", "back_psum", "x1_ready"))
        lgT_psum, lgT_ready, lg_psum, lgs_ready, lge_ready, gate_ready = (
            sem(n) for n in ("lgT_psum", "lgT_ready", "lg_psum", "lgs_ready", "lge_ready", "gate_ready"))
        h_psum, h_ready, hhi_ready, hlo_dve, hlo_pool, h_used = (
            sem(n) for n in ("h_psum", "h_ready", "hhi_ready", "hlo_dve", "hlo_pool", "h_used"))
        yT_ready, yt_psum, y_added, out_stored = (
            sem(n) for n in ("yT_ready", "yt_psum", "y_added", "out_stored"))

        block = stack.enter_context(nc.Block())

        def reached(engine, signal, value):
            if not isinstance(value, int) or value > 0:
                engine.wait_ge(signal, value)

        def hidden_split(engine, f, k):
            if k % HC == POOLS:
                engine.wait_ge(hlo_pool, f * E + k // HC + 1)
            else:
                engine.wait_ge(hlo_dve, f * (NK - E) + k + 1 - (k + HC - 1 - POOLS) // HC)


        @block.sync
        def _(sp):
            sp.dma_start(x_all[:, 0:CB, :], x[0:CB, :, :].rearrange("b s d -> s b d")).then_inc(ld_x0, 16)
            sp.dma_start(cols[:, :], pcols).then_inc(ld_consts, 16)
            sp.dma_start(wr_raw[:, :], wr).then_inc(ld_consts, 16)
            sp.dma_start(ctx[:, :], ctxT[:, 0:CT]).then_inc(ld_ctx, 16)
            sp.dma_start(w2_raw[:, :], w2).then_inc(ld_w2, 16)
            sp.dma_start(x_all[:, CB:B, :], x[CB:B, :, :].rearrange("b s d -> s b d")).then_inc(ld_x, 16)
            sp.dma_start(w1_raw[:, :], w1).then_inc(ld_w1, 16)
            sp.wait_ge(v_zeroed, 2)

            def expand_queries(nth):
                sp.wait_ge(qT_ready, nth)
                for h in range(H):
                    sp.dma_start(q_exp[HD * h:HD * (h + 1), h, :], qT[HD * h:HD * (h + 1), :]).then_inc(qexp_loaded, 16)

            def expand_values(nth):
                sp.wait_ge(vdiag_ready, nth)
                for q in range(NC):
                    sp.dma_start(v_exp[32 * q:32 * (q + 1), q, :, :, :],
                                 v_diag[32 * q:32 * (q + 1), :, :, :]).then_inc(vexp_loaded, 16)

            def load_context(split, first_token):
                sp.wait_ge(clo_ready, split)
                sp.dma_start(ctx[:, :], ctxT[:, bass.ds(first_token, CT)]).then_inc(ld_ctx, 16)

            def store(experts, first_batch):
                sp.wait_ge(y_added, experts)
                sp.dma_start(out[bass.ds(first_batch, CB), :, :].rearrange("b s d -> s b d"),
                             acc[:, :, :]).then_inc(out_stored, 16)

            def body(c, ffn=True, proj=True):
                if proj:
                    load_context(c + 1, c * CT + CT)
                    expand_queries(c + 2)
                    expand_values(c + 2)
                if ffn:
                    store(c * E + E, c * CB - CB)

            sp.sem_inc(out_stored, 16)
            sp.sem_inc(y_added, E)
            expand_values(1)
            body(0, ffn=False)
            with sp.Fori(1, CHUNKS - 1) as c:
                body(c)
            body(CHUNKS - 1, proj=False)
            store(CHUNKS * E + E, (CHUNKS - 1) * CB)
            sp.wait_ge(out_stored, (CHUNKS + 1) * 16)

        @block.gpsimd
        def _(pool):
            nc.gpsimd.memset(neg_half[:, :], -0.5).then_inc(zeroed, 1)
            nc.gpsimd.memset(kT[:, :, 0:QB], 0.0)
            nc.gpsimd.memset(vT[:, :, 0:QB], 0.0).then_inc(zeroed, 1)

            def inverse_deviation(n, var_ready, rstd_ready, veps, rstd):
                pool.wait_ge(var_ready, n + 1)
                nc.gpsimd.tensor_tensor(rstd[:, :], veps[:, :], neg_half[:, :], ALU.pow).then_inc(rstd_ready, 1)

            def context_rest(n):
                pool.wait_ge(chi_ready, n + 1)
                reached(pool, k_psum, n)
                reached(pool, v_psum, n)
                nc.gpsimd.tensor_tensor(ct_lo[:, :], ctx[:, :], ct_hi[:, :].bitcast(fp32), ALU.subtract).then_inc(clo_ready, 1)

            ln1 = (var1_ready, rstd1_ready, veps1, rstd1)
            ln2 = (var2_ready, rstd2_ready, veps2, rstd2)

            def mask_queries(b):
                pool.wait_ge(qT_ready, 1)
                nc.gpsimd.tensor_tensor(q_exp[:, :, b * S:(b + 1) * S], qT[:, None, b * S:(b + 1) * S].to_broadcast([P, H, S]),
                                        head_mask[:, :, None].to_broadcast([P, H, S]), ALU.mult).then_inc(q_masked_pool, 1)

            def first_weights_rest():
                pool.wait_ge(w1_hi_ready, 1)
                nc.gpsimd.tensor_tensor(w1_lo[:, :, :].rearrange("p k m -> p (k m)"), w1_raw[:, :],
                                        w1_hi[:, :, :].rearrange("p k m -> p (k m)").bitcast(fp32), ALU.subtract).then_inc(w1_split, 1)

            def second_weights_rest():
                pool.wait_ge(w2_hi_ready, 1)
                nc.gpsimd.tensor_tensor(w2_lo[:, :, :].rearrange("p k m -> p (k m)"), w2_raw[:, :],
                                        w2_hi[:, :, :].rearrange("p k m -> p (k m)").bitcast(fp32), ALU.subtract).then_inc(w2_split, 1)

            def hidden_lo(f, k):
                pool.wait_ge(hhi_ready, f * NK + k + 1)
                nc.gpsimd.tensor_tensor(h_lo[:, k % HRING, :], h_f[:, k % FRING, :],
                                        h_hi[:, k % HRING, :].bitcast(fp32), ALU.subtract).then_inc(hlo_pool, 1)

            pool.wait_ge(zeroed, 1)
            inverse_deviation(0, *ln1)
            nc.gpsimd.memset(v_diag[:, :, :, :], 1.0).then_inc(zeroed, 1)
            nc.gpsimd.memset(v_exp[:, 2:NC, :, :, :], 0.0).then_inc(v_zeroed, 1)
            nc.gpsimd.memset(lgT[:, :], 0.0).then_inc(zeroed, 1)
            context_rest(0)
            mask_queries(1)
            mask_queries(2)
            inverse_deviation(1, *ln1)
            mask_queries(3)
            first_weights_rest()
            context_rest(1)
            second_weights_rest()
            inverse_deviation(0, *ln2)

            def body(c, proj=True):
                f = c - 1
                for k in (POOLS, HC + POOLS):
                    hidden_lo(f, k)
                if proj:
                    inverse_deviation(c + 1, *ln1)
                    context_rest(c + 1)
                for k in (2 * HC + POOLS, 3 * HC + POOLS):
                    hidden_lo(f, k)
                inverse_deviation(c, *ln2)

            with pool.Fori(1, CHUNKS - 1) as c:
                body(c)
            body(CHUNKS - 1, proj=False)
            for k in range(POOLS, NK, HC):
                hidden_lo(CHUNKS - 1, k)

        @block.scalar
        def _(act):
            Id = ACT.Identity
            act.dma_start(cst[:, :], consts).then_inc(ld_consts, 16)
            act.dma_start(wa[:, :, :], wqkvo).then_inc(ld_wa, 16)

            def split_x(n, xT_psum, bank, hi, xhi_ready):
                act.wait_ge(xT_psum, n + 1)
                nc.scalar.activation(hi[:, :], bank[:, :], ACT.Copy).then_inc(xhi_ready, 1)

            def context_rounded(n):
                act.wait_ge(ld_ctx, n * 16 + 16)
                reached(act, v_psum, n)
                nc.scalar.activation(ct_hi[:, :], ctx[:, :], ACT.Copy).then_inc(chi_ready, 1)

            def queries(n):
                act.wait_ge(q_psum, n + 1)
                if isinstance(n, int):
                    reached(act, q_masked_dve, n)
                    reached(act, q_masked_pool, n * (CB - 1))
                else:
                    act.wait_ge(qexp_loaded, (n - 1) * 16 * H)
                reached(act, s_psum, n * CB)
                nc.scalar.activation(qT[:, :], ps_c[:, :], Id, bias=bq).then_inc(qT_ready, 1)

            def keys(n):
                act.wait_ge(k_psum, n + 1)
                nc.scalar.activation(kT[:, :, QB:SP_], ps_s[:, :].rearrange("p (b s) -> p b s", b=CB), Id,
                                     bias=bk).then_inc(kT_ready, 1)

            def values(n):
                act.wait_ge(v_psum, n + 1)
                reached(act, vdiag_ready, n)
                nc.scalar.activation(vT[:, :, QB:SP_], ps_o[:, :].rearrange("p (b s) -> p b s", b=CB), Id,
                                     bias=bv).then_inc(vT_ready, 1)

            def exponent(c, b):
                n = c * CB + b
                act.wait_ge(shifted_ready, n + 1)
                nc.scalar.activation(probs[:, b % 2, :], probs[:, b % 2, :], ACT.Exp, scale=float(HD) ** -0.5).then_inc(p_ready, 1)

            def first_half(n):
                act.wait_ge(at_psum, n + 1)
                reached(act, aT_ready, n)
                nc.scalar.activation(half[:, :].rearrange("p (g q) -> p g q", q=QB),
                                     ps_c[:, 0:2 * S].rearrange("p (g i q) -> p g i q", i=2, q=QB)[:, :, 0, :],
                                     ACT.Copy, scale=first_head).then_inc(half_ready, 1)

            def attention_rounded(c):
                act.wait_ge(aT_ready, c * CB + CB)
                nc.scalar.activation(at_hi[:, :], aT[:, :], ACT.Copy).then_inc(ahi_ready, 1)

            def projection_out(c):
                act.wait_ge(proj_psum, c + 1)
                nc.scalar.activation(oT[:, :], ps_o[:, :], Id, bias=bo).then_inc(oT_ready, 1)

            def logits_out(f):
                act.wait_ge(lgT_psum, f + 1)
                nc.scalar.activation(lgT[0:E, :], ps_c[0:E, :], Id, bias=brc).then_inc(lgT_ready, 1)

            def gate_exponent(f):
                act.wait_ge(lgs_ready, f + 1)
                nc.scalar.activation(lge[:, :, :], lgs[:, :, :], ACT.Exp).then_inc(lge_ready, 1)

            def hidden(f, k):
                act.wait_ge(h_psum, f * NK + k + 1)
                if k >= FRING:
                    hidden_split(act, f, k - FRING)
                nc.scalar.activation(h_f[:, k % FRING, :], ps_h[k % 2][:, :], ACT.Gelu,
                                     bias=b1c[:, k:k + 1]).then_inc(h_ready, 1)

            def hidden_rounded(f, k):
                act.wait_ge(h_ready, f * NK + k + 1)
                if k >= HRING:
                    act.wait_ge(h_used, f * NK + k + 1 - HRING)
                nc.scalar.activation(h_hi[:, k % HRING, :], h_f[:, k % FRING, :], ACT.Copy).then_inc(hhi_ready, 1)

            def expert_out(f, e):
                act.wait_ge(h_used, f * NK + (e + 1) * HC)
                if e > 0:
                    act.wait_ge(yt_psum, f * E + e)
                nc.scalar.activation(yT[:, :], ps_y[e % 2][:, :], Id, bias=kappa[:, e:e + 1]).then_inc(yT_ready, 1)

            def weights_first():
                act.wait_ge(ld_wa, 16)
                nc.scalar.activation(wa_hi[:, :, :], wa[:, :, :], ACT.Copy)
                act.wait_ge(ld_consts, 48)
                nc.scalar.activation(wr_hi[:, :], wr_raw[:, :], ACT.Copy).then_inc(wa_hi_ready, 1)

            def second_weights_rounded():
                act.wait_ge(ld_w2, 16)
                nc.scalar.activation(w2_hi[:, :, :].rearrange("p k m -> p (k m)"), w2_raw[:, :], ACT.Copy).then_inc(w2_hi_ready, 1)

            def first_weights_rounded():
                act.wait_ge(ld_w1, 16)
                nc.scalar.activation(w1_hi[:, :, :].rearrange("p k m -> p (k m)"), w1_raw[:, :], ACT.Copy).then_inc(w1_hi_ready, 1)

            def body(c, ffn=True, proj=True):
                f, n = c - 1, c * CB

                def gelu(*ks):
                    for k in ks if ffn else ():
                        hidden(f, k)

                def rounded(*ks):
                    for k in ks if ffn else ():
                        hidden_rounded(f, k)

                def y_out(*es):
                    for e in es if ffn else ():
                        expert_out(f, e)

                gelu(0, 1)
                rounded(0)
                gelu(2)
                rounded(1)
                gelu(3)
                rounded(2)
                gelu(4)
                exponent(c, 0)
                rounded(3, 4)
                if ffn:
                    logits_out(f)
                exponent(c, 1)
                if not ffn:
                    first_weights_rounded()
                    second_weights_rounded()
                gelu(5, 6)
                rounded(5)
                first_half(n + 0)
                rounded(6)
                gelu(7, 8)
                rounded(7)
                if proj:
                    context_rounded(c + 1)
                gelu(9)
                first_half(n + 1)
                exponent(c, 2)
                if proj:
                    split_x(c + 1, xT1_psum, ps_c, xt_hi, xhi1_ready)
                exponent(c, 3)
                rounded(8)
                if ffn:
                    gate_exponent(f)
                gelu(10)
                if proj:
                    queries(c + 1)
                y_out(0)
                rounded(9)
                first_half(n + 2)
                gelu(11)
                rounded(10)
                y_out(1)
                first_half(n + 3)
                rounded(11)
                attention_rounded(c)
                gelu(12)
                if proj:
                    keys(c + 1)
                rounded(12)
                projection_out(c)
                gelu(13)
                rounded(13)
                gelu(14, 15)
                rounded(14, 15)
                y_out(2, 3)
                split_x(c, xT2_psum, ps_t, x2_hi, xhi2_ready)
                if proj:
                    values(c + 1)

            def last_experts(f):
                def gelu(*ks):
                    for k in ks:
                        hidden(f, k)

                def rounded(*ks):
                    for k in ks:
                        hidden_rounded(f, k)

                def y_out(*es):
                    for e in es:
                        expert_out(f, e)

                gelu(0)
                rounded(0)
                gelu(1)
                logits_out(f)
                gelu(2)
                rounded(1)
                gelu(3)
                rounded(2)
                gelu(4)
                rounded(3)
                gelu(5)
                rounded(4)
                gelu(6)
                rounded(5)
                gelu(7)
                rounded(6)
                gelu(8)
                rounded(7)
                gate_exponent(f)
                gelu(9)
                rounded(8)
                gelu(10)
                y_out(0)
                rounded(9)
                gelu(11)
                rounded(10)
                gelu(12)
                rounded(11)
                gelu(13)
                rounded(12)
                y_out(1)
                rounded(13)
                gelu(14)
                rounded(14)
                gelu(15)
                rounded(15)
                y_out(2, 3)

            weights_first()
            nc.scalar.activation(gelu_b1[:, :], b1c, ACT.Gelu).then_inc(gelu_b1_ready, 1)
            act.wait_ge(zeroed, 2)
            split_x(0, xT1_psum, ps_c, xt_hi, xhi1_ready)
            context_rounded(0)
            queries(0)
            keys(0)
            values(0)
            body(0, ffn=False)
            act.wait_ge(zeroed, 4)
            act.wait_ge(kappa_ready, 1)
            with act.Fori(1, CHUNKS - 1) as c:
                body(c)
            body(CHUNKS - 1, proj=False)
            last_experts(CHUNKS - 1)

        @block.vector
        def _(dve):
            V = nc.vector

            def link(ins, chain, value):
                ins.then_inc(chain, 1)
                dve.wait_ge(chain, value)

            def weights_first():
                dve.wait_ge(wa_hi_ready, 1)
                V.tensor_tensor(wa_lo[:, :, :], wa[:, :, :], wa_hi[:, :, :].bitcast(fp32), ALU.subtract)
                V.tensor_tensor(wr_lo[:, :], wr_raw[:, :], wr_hi[:, :].bitcast(fp32), ALU.subtract).then_inc(wa_split, 1)

            def mask_queries(b):
                dve.wait_ge(qT_ready, 1)
                V.tensor_tensor(q_exp[:, :, b * S:(b + 1) * S], qT[:, None, b * S:(b + 1) * S].to_broadcast([P, H, S]),
                                head_mask[:, :, None].to_broadcast([P, H, S]), ALU.mult).then_inc(q_masked_dve, 1)

            def constants_of_experts():
                dve.wait_ge(d_psum, E)
                V.tensor_reduce(csum[:, 0:1], y0[:, 0:E], X, ALU.add)
                link(V.tensor_reduce(csum[:, 1:2], b2c, X, ALU.add), setup_chain, 1)
                link(V.tensor_tensor(csum[:, 0:1], csum[:, 0:1], csum[:, 1:2], ALU.add), setup_chain, 2)
                V.tensor_scalar(kappa[:, :], y0[:, 0:E], -1.0, csum[:, 0:1], ALU.mult, ALU.add).then_inc(kappa_ready, 1)

            def statistics(n, src, chain, var_ready, mv, veps):
                for b in range(CB):
                    last = V.bn_stats(stats[:, b, :], src[b])
                link(last, chain, n * 2 + 1)
                V.memset(fence[:, 0:1], 0.0)
                for b in range(CB):
                    last = V.bn_aggr(mv[:, b, :], stats[:, b, :])
                link(last, chain, n * 2 + 2)
                V.tensor_scalar(veps[:, :], mv[:, :, 1], EPS, None, ALU.add).then_inc(var_ready, 1)

            def normalized(n, src, rstd_ready, xT_psum, mv, rstd, xn, xn_ready):
                dve.wait_ge(rstd_ready, n + 1)
                reached(dve, xT_psum, n)
                for b in range(CB):
                    last = V.tensor_scalar(xn[:, b, :], src[b], mv[:, b, 0:1], rstd[:, b:b + 1],
                                           ALU.subtract, ALU.mult)
                last.then_inc(xn_ready, 1)

            def x_tiles(n):
                return [x_all[:, bass.ds(n * CB + b, 1), :].rearrange("p o d -> p (o d)") for b in range(CB)]

            def statistics1(n):
                statistics(n, x_tiles(n), ln1_chain, var1_ready, mv1, veps1)

            def normalized1(n):
                normalized(n, x_tiles(n), rstd1_ready, xT1_psum, mv1, rstd1, xn1, xn1_ready)

            def windows(t, b):
                a = t[:, b, 0:KW]
                return bass.AP(a.tensor, a.offset, [list(a.ap[0]), [QB, NQB], [1, KW]])

            def values_in(n):
                dve.wait_ge(vT_ready, n + 1)
                reached(dve, vexp_loaded, n * 16 * NC)
                reached(dve, o_psum, n * CB)
                for b in range(CB):
                    last = V.transpose(v_diag[:, b * NQB:(b + 1) * NQB, :, 0:2 * HD], windows(vT, b))
                last.then_inc(vdiag_ready, 1)

            def split_lo(n, bank, hi, lo, xhi_ready, xlo_ready):
                dve.wait_ge(xhi_ready, n + 1)
                V.tensor_tensor(lo[:, :], bank[:, :], hi[:, :].bitcast(fp32), ALU.subtract).then_inc(xlo_ready, 1)

            x1_tiles = [x1[:, b, :] for b in range(CB)]

            def scores_out(c, b):
                n = c * CB + b
                dve.wait_ge(s_psum, n + 1)
                reached(dve, sc_psum, n - 1)
                V.tensor_tensor(sT[:, b % 2, :].rearrange("p (u h q) -> p u h q", u=QUADS, q=QB),
                                ps_s[:, :].rearrange("p (u h q) -> p u h q", u=QUADS, q=QB),
                                mask[:, :, None, :].to_broadcast([P, QUADS, H, QB]), ALU.add).then_inc(sT_ready, 1)

            def shift(c, b):
                n = c * CB + b
                dve.wait_ge(sc_psum, n + 1)
                blocks = ps_t[:, :].rearrange("p (g k) -> p g k", k=KW)
                link(V.tensor_reduce(smax[:, :], blocks, X, ALU.max), max_chain, n + 1)
                reached(dve, pT_ready, n - 1)
                V.tensor_tensor(probs[:, b % 2, :].rearrange("p (g k) -> p g k", k=KW), blocks,
                                smax[:, :, None].to_broadcast([P, 16, KW]), ALU.subtract).then_inc(shifted_ready, 1)

            def keys_first(c, b):
                n = c * CB + b
                dve.wait_ge(p_ready, n + 1)
                reached(dve, o_psum, n - 1)
                V.transpose(pT[:, b % 2, :], probs[:, b % 2, :]).then_inc(pT_ready, 1)

            def normalize(n):
                dve.wait_ge(o_psum, n + 1)
                o = ps_o[:, 0:16 * VW].rearrange("p (g v) -> p g v", v=VW)
                link(V.reciprocal(rden[:, :], o[:, :, 2 * HD]), den_chain, n + 1)
                reached(dve, at_psum, n)
                V.tensor_tensor(att[:, :].rearrange("p (g v) -> p g v", v=2 * HD), o[:, :, 0:2 * HD],
                                rden[:, :, None].to_broadcast([P, 16, 2 * HD]), ALU.mult).then_inc(att_ready, 1)

            def second_half(c, b):
                n = c * CB + b
                dve.wait_ge(half_ready, n + 1)
                reached(dve, alo_ready, c)
                V.scalar_tensor_tensor(aT[:, b * S:(b + 1) * S].rearrange("p (g q) -> p g q", q=QB),
                                       ps_c[:, 0:2 * S].rearrange("p (g i q) -> p g i q", i=2, q=QB)[:, :, 1, :],
                                       second_head, half[:, :].rearrange("p (g q) -> p g q", q=QB),
                                       ALU.mult, ALU.add).then_inc(aT_ready, 1)

            def attention_rest(c):
                dve.wait_ge(ahi_ready, c + 1)
                V.tensor_tensor(at_lo[:, :], aT[:, :], at_hi[:, :].bitcast(fp32), ALU.subtract).then_inc(alo_ready, 1)

            def residual(c, ffn):
                dve.wait_ge(back_psum, c + 1)
                if ffn:
                    dve.wait_ge(y_added, c * E + 1)
                V.tensor_tensor(x1[:, :, :], ps_t[:, :].rearrange("p (b d) -> p b d", b=CB),
                                x_all[:, bass.ds(c * CB, CB), :], ALU.add).then_inc(x1_ready, 1)
                dve.wait_ge(x1_ready, c + 1)

            def gate_logits(f):
                dve.wait_ge(lg_psum, f + 1)
                link(V.tensor_copy(lg[:, :, :], ps_c[:, :].rearrange("p (b e) -> p b e", b=CB)[:, :, 0:E]),
                     gate_chain, f * 9 + 1)
                link(V.tensor_reduce(lmax[:, :], lg[:, :, :], X, ALU.max), gate_chain, f * 9 + 2)
                V.tensor_tensor(lgs[:, :, :], lg[:, :, :], lmax[:, :, None].to_broadcast([P, CB, E]),
                                ALU.subtract).then_inc(lgs_ready, 1)

            def gate_ranks(f):
                others = lg[:, :, None, :].to_broadcast([P, CB, E, E])
                own = lg[:, :, :, None].to_broadcast([P, CB, E, E])
                V.tensor_tensor(gt[:, :, :, :], others, own, ALU.is_gt)
                link(V.tensor_tensor(eq[:, :, :, :], others, own, ALU.is_equal), gate_chain, f * 9 + 3)
                link(V.tensor_tensor(eq[:, :, :, :], eq[:, :, :, :], lower[:, None, :, :].to_broadcast([P, CB, E, E]),
                                     ALU.mult), gate_chain, f * 9 + 4)
                link(V.tensor_tensor(gt[:, :, :, :], gt[:, :, :, :], eq[:, :, :, :], ALU.add), gate_chain, f * 9 + 5)
                link(V.tensor_reduce(rank[:, :, :], gt[:, :, :, :], X, ALU.add), gate_chain, f * 9 + 6)

            def gate_weights(f):
                dve.wait_ge(lge_ready, f + 1)
                link(V.scalar_tensor_tensor(gsel[:, :, :], rank[:, :, :], 2.0, lge[:, :, :], ALU.is_lt, ALU.mult),
                     gate_chain, f * 9 + 7)
                link(V.tensor_reduce(gsum[:, :], gsel[:, :, :], X, ALU.add), gate_chain, f * 9 + 8)
                link(V.reciprocal(gsum[:, :], gsum[:, :]), gate_chain, f * 9 + 9)
                V.tensor_tensor(gate[:, :, :], gsel[:, :, :], gsum[:, :, None].to_broadcast([P, CB, E]),
                                ALU.mult).then_inc(gate_ready, 1)

            def hidden_lo(f, k):
                dve.wait_ge(hhi_ready, f * NK + k + 1)
                V.tensor_tensor(h_lo[:, k % HRING, :], h_f[:, k % FRING, :], h_hi[:, k % HRING, :].bitcast(fp32),
                                ALU.subtract).then_inc(hlo_dve, 1)

            def add_expert(f, e):
                dve.wait_ge(yt_psum, f * E + e + 1)
                if e == 0:
                    dve.wait_ge(gate_ready, f + 1)
                    dve.wait_ge(out_stored, f * 16 + 16)
                else:
                    dve.wait_ge(y_added, f * E + E + e)
                before = x1 if e == 0 else acc
                for b in range(CB):
                    last = V.scalar_tensor_tensor(acc[:, b, :], ps_s[:, b * S:(b + 1) * S], gate[:, b, e:e + 1],
                                                  before[:, b, :], ALU.mult, ALU.add)
                last.then_inc(y_added, 1)

            def body(c, ffn=True, proj=True):
                f, n = c - 1, c * CB

                def lo(*ks):
                    for k in ks if ffn else ():
                        hidden_lo(f, k)

                def add(*es):
                    for e in es if ffn else ():
                        add_expert(f, e)

                scores_out(c, 0)
                lo(0)
                if proj:
                    statistics1(c + 1)
                shift(c, 0)
                scores_out(c, 1)
                lo(2)
                keys_first(c, 0)
                shift(c, 1)
                scores_out(c, 2)
                normalize(n + 0)
                lo(3)
                if ffn:
                    gate_logits(f)
                keys_first(c, 1)
                lo(4)
                shift(c, 2)
                scores_out(c, 3)
                second_half(c, 0)
                normalize(n + 1)
                lo(6)
                if proj:
                    normalized1(c + 1)
                second_half(c, 1)
                shift(c, 3)
                keys_first(c, 2)
                lo(7)
                if proj:
                    split_lo(c + 1, ps_c, xt_hi, xt_lo, xhi1_ready, xlo1_ready)
                keys_first(c, 3)
                normalize(n + 2)
                if ffn:
                    gate_ranks(f)
                lo(8)
                if ffn:
                    gate_weights(f)
                normalize(n + 3)
                second_half(c, 2)
                add(0)
                second_half(c, 3)
                lo(10)
                attention_rest(c)
                lo(11, 12)
                add(1)
                residual(c, ffn)
                statistics(c, x1_tiles, ln2_chain, var2_ready, mv2, veps2)
                if not ffn:
                    constants_of_experts()
                lo(14, 15)
                normalized(c, x1_tiles, rstd2_ready, xT2_psum, mv2, rstd2, xn2, xn2_ready)
                add(2)
                split_lo(c, ps_t, x2_hi, x2_lo, xhi2_ready, xlo2_ready)
                add(3)
                if proj:
                    values_in(c + 1)

            def last_experts(f):
                def lo(*ks):
                    for k in ks:
                        hidden_lo(f, k)

                def add(*es):
                    for e in es:
                        add_expert(f, e)

                lo(0, 2, 3, 4)
                gate_logits(f)
                lo(6)
                gate_ranks(f)
                lo(7, 8)
                gate_weights(f)
                lo(10, 11)
                add(0)
                lo(12)
                add(1)
                lo(14, 15)
                add(2, 3)

            V.memset(idle[:, :], 0.0).then_inc(idle_zeroed, 1)
            V.memset(v_exp[:, 0:2, :, :, :], 0.0).then_inc(v_zeroed, 1)
            dve.wait_ge(ld_x0, 16)
            statistics1(0)
            normalized1(0)
            weights_first()
            split_lo(0, ps_c, xt_hi, xt_lo, xhi1_ready, xlo1_ready)
            dve.wait_ge(ld_consts, 48)
            mask_queries(0)
            dve.wait_ge(zeroed, 3)
            values_in(0)
            dve.wait_ge(ld_x, 16)
            body(0, ffn=False)
            with dve.Fori(1, CHUNKS - 1) as c:
                body(c)
            body(CHUNKS - 1, proj=False)
            last_experts(CHUNKS - 1)

        @block.tensor
        def _(pe):
            mm = nc.tensor.matmul

            def split_mm(ps, w_hi, w_lo, r_hi, r_lo, start=True, stop=True):
                mm(ps, w_hi, r_hi, start=start, stop=False)
                mm(ps, w_hi, r_lo, start=False, stop=False)
                return mm(ps, w_lo, r_hi, start=False, stop=stop)

            def wake(products):
                for _ in range(products):
                    mm(y1[:, :], idle[:, 0:P], idle[:, :], start=True, stop=True)

            def transposes(bank, src):
                for b in range(CB):
                    last = nc.tensor.transpose(bank[:, b * P:(b + 1) * P], src(b), ident)
                return last

            def constant_of_expert(e):
                pe.wait_ge(gelu_b1_ready, 1)
                pe.wait_ge(ld_w2, 16)
                for k in range(HC):
                    i = e * HC + k
                    last = mm(y0[:, e:e + 1], w2_raw[:, i * P:(i + 1) * P], gelu_b1[:, i:i + 1],
                              start=(k == 0), stop=(k == HC - 1))
                last.then_inc(d_psum, 1)


            def input_columns(n):
                pe.wait_ge(xn1_ready, n + 1)
                reached(pe, aT_ready, n * CB - CB + 2)
                transposes(ps_c, lambda b: xn1[:, b, :]).then_inc(xT1_psum, 1)

            def queries(n):
                pe.wait_ge(xlo1_ready, n + 1)
                split_mm(ps_c[:, :], wa_hi[:, 0, :], wa_lo[:, 0, :], xt_hi[:, :], xt_lo[:, :]).then_inc(q_psum, 1)

            def keys(n, ffn=False):
                pe.wait_ge(clo_ready, n + 1)
                if ffn:
                    pe.wait_ge(y_added, (n - 1) * E + 1)
                else:
                    reached(pe, sT_ready, n * CB)
                split_mm(ps_s[:, :], wa_hi[:, 1, :], wa_lo[:, 1, :], ct_hi[:, :], ct_lo[:, :]).then_inc(k_psum, 1)

            def values(n):
                pe.wait_ge(clo_ready, n + 1)
                reached(pe, oT_ready, n)
                split_mm(ps_o[:, :], wa_hi[:, 2, :], wa_lo[:, 2, :], ct_hi[:, :], ct_lo[:, :]).then_inc(v_psum, 1)

            def scores(c, b, ffn):
                n = c * CB + b
                if b == 0:
                    pe.wait_ge(kT_ready, c + 1)
                    if ffn:
                        pe.wait_ge(qexp_loaded, c * 16 * H)
                    if ffn:
                        pe.wait_ge(y_added, c * E)
                else:
                    pe.wait_ge(sT_ready, n)
                if not ffn:
                    if b == 0:
                        pe.wait_ge(q_masked_dve, 1)
                    else:
                        pe.wait_ge(q_masked_pool, b)
                for quad in range(QUADS):
                    for j in range(4):
                        t = QB * (4 * quad + j)
                        last = mm(ps_s[32 * j:32 * (j + 1), quad * 256:(quad + 1) * 256], kT[:, b, t:t + KW],
                                  q_exp[:, :, b * S + t:b * S + t + QB], start=True, stop=True,
                                  skip_group_check=True)
                last.then_inc(s_psum, 1)

            def score_rows(c, b):
                n = c * CB + b
                pe.wait_ge(sT_ready, n + 1)
                if b > 0:
                    pe.wait_ge(shifted_ready, n)
                transposes(ps_t, lambda i: sT[:, b % 2, i * P:(i + 1) * P]).then_inc(sc_psum, 1)

            def attend(c, b):
                n = c * CB + b
                if b == 0:
                    pe.wait_ge(vexp_loaded, (c + 1) * 16 * NC)
                pe.wait_ge(pT_ready, n + 1)
                reached(pe, att_ready, n)
                for quad in range(QUADS):
                    for g in range(2):
                        for j in range(4):
                            i = quad * 2 + g
                            last = mm(ps_o[32 * j:32 * (j + 1), i * NC * VW:(i + 1) * NC * VW],
                                      pT[:, b % 2, (4 * i + j) * KW:(4 * i + j + 1) * KW],
                                      v_exp[:, :, b * NQB + 4 * quad + j, g, :], start=True, stop=True,
                                      skip_group_check=True)
                last.then_inc(o_psum, 1)

            def attention_columns(c, b, ffn, proj):
                n = c * CB + b
                pe.wait_ge(att_ready, n + 1)
                if b == 0 and ffn:
                    pe.wait_ge(lgs_ready, c)
                elif b == 2 and proj:
                    pe.wait_ge(qT_ready, c + 2)
                elif b > 0:
                    pe.wait_ge(aT_ready, n)
                for quad in range(QUADS):
                    last = nc.tensor.transpose(ps_c[:, quad * P:(quad + 1) * P], att[:, quad * P:(quad + 1) * P], ident)
                last.then_inc(at_psum, 1)

            def projection(c):
                pe.wait_ge(alo_ready, c + 1)
                split_mm(ps_o[:, :], wa_hi[:, 3, :], wa_lo[:, 3, :], at_hi[:, :], at_lo[:, :]).then_inc(proj_psum, 1)

            def back(c):
                pe.wait_ge(oT_ready, c + 1)
                transposes(ps_t, lambda b: oT[:, b * P:(b + 1) * P]).then_inc(back_psum, 1)

            def normalized_columns(c):
                pe.wait_ge(xn2_ready, c + 1)
                transposes(ps_t, lambda b: xn2[:, b, :]).then_inc(xT2_psum, 1)

            def logits(f):
                pe.wait_ge(xlo2_ready, f + 1)
                split_mm(ps_c[0:E, :], wr_hi[:, :], wr_lo[:, :], x2_hi[:, :], x2_lo[:, :]).then_inc(lgT_psum, 1)

            def logit_rows(f):
                pe.wait_ge(lgT_ready, f + 1)
                transposes(ps_c, lambda b: lgT[:, b * P:(b + 1) * P]).then_inc(lg_psum, 1)

            def first_layer(f, k):
                if k == 0:
                    pe.wait_ge(xlo2_ready, f + 1)
                if k >= 2:
                    pe.wait_ge(h_ready, f * NK + k - 1)
                split_mm(ps_h[k % 2][:, :], w1_hi[:, k, :], w1_lo[:, k, :], x2_hi[:, :], x2_lo[:, :]).then_inc(h_psum, 1)

            def second_layer(f, k):
                e = k // HC
                if k % HC == 0 and e >= 2:
                    pe.wait_ge(yT_ready, f * E + e - 1)
                hidden_split(pe, f, k)
                r = k % HRING
                split_mm(ps_y[e % 2][:, :], w2_hi[:, k, :], w2_lo[:, k, :], h_hi[:, r, :], h_lo[:, r, :],
                         start=(k % HC == 0), stop=(k % HC == HC - 1)).then_inc(h_used, 1)

            def expert_rows(f, e, proj):
                pe.wait_ge(yT_ready, f * E + e + 1)
                if e == 1 and proj:
                    pe.wait_ge(kT_ready, f + 3)
                pe.wait_ge(y_added, f * E + E + e)
                transposes(ps_s, lambda b: yT[:, b * P:(b + 1) * P]).then_inc(yt_psum, 1)

            def body(c, ffn=True, proj=True):
                f = c - 1

                def l1(*ks):
                    for k in ks if ffn else ():
                        first_layer(f, k)

                def l2(*ks):
                    for k in ks if ffn else ():
                        second_layer(f, k)

                def rows(*es):
                    for e in es if ffn else ():
                        expert_rows(f, e, proj)

                l1(0, 1)
                scores(c, 0, ffn)
                l1(2, 3)
                score_rows(c, 0)
                l1(4)
                if ffn:
                    logits(f)
                scores(c, 1, ffn)
                if not ffn:
                    constant_of_expert(1)
                l1(5, 6)
                score_rows(c, 1)
                scores(c, 2, ffn)
                if not ffn:
                    wake(3)
                attend(c, 0)
                l2(0)
                if ffn:
                    logit_rows(f)
                score_rows(c, 2)
                scores(c, 3, ffn)
                attention_columns(c, 0, ffn, proj)
                if not ffn:
                    wake(3)
                l1(7, 8)
                attend(c, 1)
                l2(1)
                l1(9)
                score_rows(c, 3)
                attention_columns(c, 1, ffn, proj)
                if not ffn:
                    wake(4)
                l1(10)
                l2(2, 3)
                if proj:
                    input_columns(c + 1)
                l1(11)
                l2(4)
                attend(c, 2)
                l2(5)
                if proj:
                    queries(c + 1)
                l2(6)
                attend(c, 3)
                attention_columns(c, 2, ffn, proj)
                l2(7)
                rows(0)
                l1(12)
                attention_columns(c, 3, ffn, proj)
                if not ffn:
                    constant_of_expert(2)
                    wake(4)
                l1(13)
                if proj:
                    keys(c + 1, ffn)
                l2(8, 9)
                projection(c)
                if not ffn:
                    constant_of_expert(3)
                rows(1)
                l1(14)
                back(c)
                if not ffn:
                    wake(16)
                l1(15)
                l2(10, 11, 12, 13, 14)
                rows(2)
                l2(15)
                normalized_columns(c)
                if proj:
                    values(c + 1)
                rows(3)

            def last_experts(f):
                def l1(*ks):
                    for k in ks:
                        first_layer(f, k)

                def l2(*ks):
                    for k in ks:
                        second_layer(f, k)

                def rows(*es):
                    for e in es:
                        expert_rows(f, e, False)

                l1(0, 1)
                logits(f)
                l1(2, 3, 4, 5)
                l2(0)
                l1(6, 7)
                l2(1)
                l1(8)
                l2(2)
                logit_rows(f)
                l2(3)
                l1(9)
                l2(4, 5, 6)
                l1(10, 11)
                l2(7)
                l1(12)
                rows(0)
                l2(8)
                l1(13)
                l2(9)
                l1(14, 15)
                l2(10)
                rows(1)
                l2(11, 12, 13, 14)
                rows(2)
                l2(15)
                rows(3)

            pe.wait_ge(idle_zeroed, 1)
            wake(15)
            pe.wait_ge(ld_consts, 48)
            input_columns(0)
            pe.wait_ge(wa_split, 1)
            queries(0)
            keys(0)
            values(0)
            constant_of_expert(0)
            wake(3)
            body(0, ffn=False)
            pe.wait_ge(w1_split, 1)
            pe.wait_ge(w2_split, 1)
            pe.wait_ge(kappa_ready, 1)
            with pe.Fori(1, CHUNKS - 1) as c:
                body(c)
            body(CHUNKS - 1, proj=False)
            last_experts(CHUNKS - 1)


_SHAPES = {"x": (B, S, D), "ctxT": (D, B * S), "wqkvo": (D, 4, D), "w1": (D, NK * P), "w2": (P, NK * D),
           "pcols": (P, 28), "wr": (D, E), "consts": (P, CONSTS)}


def constants():
    import numpy as np
    c = np.zeros((P, CONSTS), np.float32)
    c[:, 0:128] = np.eye(P)
    head = (np.arange(P) // HD) % 2
    c[:, 128] = head == 0
    c[:, 129] = head == 1
    c[:, 130:146] = (np.arange(E)[None, :] < np.arange(E)[:, None]).reshape(1, 16)
    for quad in range(QUADS):
        for q in range(QB):
            for j in range(4):
                last = min(q + W, 2 * q + 1) if quad == 0 and j == 0 else q + W
                for k in range(KW):
                    if not q + 1 <= k <= last:
                        c[j * KW + k, 146 + quad * QB + q] = -1e30
    c[np.arange(P), 178 + np.arange(P) // HD] = 1.0
    return c


def kernel(**inputs):
    import numpy as np
    import concourse.bacc as bacc
    from concourse import mybir as mb
    from concourse.bass_utils import run_bass_kernel_spmd

    a = {k: np.ascontiguousarray(v) for k, v in inputs.items()}
    order = np.arange(D).reshape(2, NC, 2, HD).transpose(1, 0, 2, 3).reshape(-1)
    wv, bv = a["L0_xattn_Wv"][order, :], a["L0_xattn_bv"][order]
    br = np.zeros(P, np.float32)
    br[:E] = a["L0_ffn_br"]
    arrays = {
        "x": a["x"],
        "ctxT": a["ctx_1024"].transpose(2, 0, 1).reshape(D, B * S),
        "wqkvo": np.stack([a["L0_xattn_Wq"].T, a["L0_xattn_Wk"].T, wv.T, a["L0_xattn_Wo"].T], axis=1),
        "w1": a["L0_ffn_w1"].reshape(E, D, HC, P).transpose(1, 0, 2, 3).reshape(D, NK * P),
        "w2": a["L0_ffn_w2"].reshape(E, HC, P, D).transpose(2, 0, 1, 3).reshape(P, NK * D),
        "pcols": np.concatenate([
            np.stack([a["L0_xattn_bq"], a["L0_xattn_bk"], bv, a["L0_xattn_bo"]], axis=1),
            a["L0_ffn_b1"].reshape(NK, P).T, a["L0_ffn_b2"].T, br[:, None], np.zeros((P, 3), np.float32)], axis=1),
        "wr": a["L0_ffn_wr"],
        "consts": constants(),
    }
    arrays = {k: np.ascontiguousarray(v) for k, v in arrays.items()}
    nc = bacc.Bacc("TRN2", target_bir_lowering=False, num_devices=1)
    aps = [nc.dram_tensor(f"in_{k}", arrays[k].shape, mb.dt.from_np(arrays[k].dtype), kind="ExternalInput").ap()
           for k in _SHAPES]
    out = nc.dram_tensor("out", (B, S, D), mb.dt.float32, kind="ExternalOutput").ap()
    xattn_ffn_kernel(nc, *aps, out)
    r = run_bass_kernel_spmd(nc, [{f"in_{k}": v for k, v in arrays.items()}], core_ids=[0])
    return r.results[0]["out"]
```
